# Optimizing a Trainium2 kernel written in Bass

```python
import numpy as np
import jax
import jax.numpy as jnp

def _softmax(x, axis=-1):
    return jax.nn.softmax(x, axis=axis)

def _gelu(x):
    return jax.nn.gelu(x, approximate=True)

def _silu(x):
    return jax.nn.silu(x)

def _sigmoid(x):
    return jax.nn.sigmoid(x)

def _layernorm(x, axis=-1, eps=1e-05):
    m = jnp.mean(x, axis=axis, keepdims=True)
    v = jnp.var(x, axis=axis, keepdims=True)
    return (x - m) / jnp.sqrt(v + eps)

def _scatter_add(tgt, idx, src, axis=0):
    return tgt.at[idx].add(src)

def _segment_sum(src, seg, n):
    return jax.ops.segment_sum(src, seg, n)
kernel_name = 'mk_xattn_ffn_d2_seqx_r4_18616d'

def setup_inputs(seed: int=0):
    np.random.seed(seed)
    _w = jnp.asarray

    def _rec_inputs():
        import jax
        import jax.numpy as jnp
        _rk = jax.random.key(seed)
        x = 7.22e-05 + 1 * jax.random.normal(jax.random.fold_in(_rk, 1), (32, 100, 256), jnp.float32)
        _lenS = 100 - jax.random.randint(jax.random.fold_in(_rk, 7), (32,), 0, max(1, 100 // 4) + 1, jnp.int32)
        _lenS2 = 361 - jax.random.randint(jax.random.fold_in(_rk, 8), (32,), 0, max(1, 361 // 4) + 1, jnp.int32)
        _ctx_1024P = jax.random.normal(jax.random.fold_in(_rk, 11), (32, 16, 256), jnp.float32)
        _ctx_1024c = jax.random.dirichlet(jax.random.fold_in(_rk, 511), 0.3 * jnp.ones((16,), jnp.float32), (32, 361))
        _ctx_1024t = jnp.einsum('bsk,bkd->bsd', _ctx_1024c, _ctx_1024P)
        _ctx_1024t = _ctx_1024t * jax.lax.rsqrt(jnp.mean(jnp.square(_ctx_1024t)) + 1e-12) * 0.953939
        ctx_1024 = 4.13588e-05 + 0.999923 * (_ctx_1024t + 0.3 * jax.random.normal(jax.random.fold_in(_rk, 611), (32, 361, 256), jnp.float32))
        return (x, ctx_1024)
    x, ctx_1024 = _rec_inputs()

    def _L0_xattn_setup():
        import jax, jax.numpy as jnp
        import numpy as np
        B, LQ, LK, D = (4, 512, 512, 256)
        H = 16
        HD = D // H
        key = jax.random.key(seed)
        ks = jax.random.split(key, 4)
        std = 0.02
        return {'x': jax.random.normal(ks[0], (B, LQ, D), dtype=jnp.float32), 'text_input': jax.random.normal(ks[1], (B, LK, D), dtype=jnp.float32), 'Wq': jax.random.normal(ks[2], (D, D), dtype=jnp.float32) * std, 'bq': jnp.zeros((D,), dtype=jnp.float32), 'Wkv': jax.random.normal(ks[3], (D, 2 * D), dtype=jnp.float32) * std, 'bkv': jnp.zeros((2 * D,), dtype=jnp.float32)}
    _L0_xattn_all = _L0_xattn_setup()
    _L0_xattn_in = {k: v for k, v in _L0_xattn_all.items() if k in ('Wq', 'bq', 'Wkv', 'bkv')}
    del _L0_xattn_all

    def _L0_ffn_setup():
        import jax, jax.numpy as jnp
        import numpy as np
        E, D, F = (8, 256, 1024)
        LN_EPS = 1e-05
        key = jax.random.key(seed)
        k = jax.random.split(key, 8)
        x = jax.random.normal(k[0], (4, 512, D), jnp.float32)
        centroids = jax.random.normal(k[1], (E, D), jnp.float32) * 0.1
        ln_g = jnp.ones((E, D), jnp.float32)
        ln_b = jnp.zeros((E, D), jnp.float32)
        w1 = jax.random.normal(k[2], (E, F, D), jnp.float32) * (1.0 / np.sqrt(D))
        b1 = jnp.zeros((E, F), jnp.float32)
        w2 = jax.random.normal(k[3], (E, D, F), jnp.float32) * (1.0 / np.sqrt(F))
        b2 = jnp.zeros((E, D), jnp.float32)
        return {'input_features': x, 'centroids': centroids, 'ln_g': ln_g, 'ln_b': ln_b, 'w1': w1, 'b1': b1, 'w2': w2, 'b2': b2}
    _L0_ffn_all = _L0_ffn_setup()
    _L0_ffn_in = {k: v for k, v in _L0_ffn_all.items() if k in ('centroids', 'ln_g', 'ln_b', 'w1', 'b1', 'w2', 'b2')}
    del _L0_ffn_all

    def _L1_xattn_setup():
        import jax, jax.numpy as jnp
        import numpy as np
        DIM_Q = 256
        DIM_V = 256
        NUM_HEADS = 8
        LN_EPS = 1e-05

        def _layernorm(x, gamma, beta):
            mu = jnp.mean(x, axis=-1, keepdims=True)
            var = jnp.mean((x - mu) ** 2, axis=-1, keepdims=True)
            return (x - mu) * jax.lax.rsqrt(var + LN_EPS) * gamma + beta
        key = jax.random.key(seed)
        ks = jax.random.split(key, 12)
        B, NQ, NK = (4, 256, 1024)
        s_in = 1.0 / np.sqrt(DIM_Q)
        s_v = 1.0 / np.sqrt(DIM_V)
        return {'Q': jax.random.normal(ks[0], (B, NQ, DIM_Q), dtype=jnp.float32), 'K': jax.random.normal(ks[1], (B, NK, DIM_Q), dtype=jnp.float32), 'Wq': jax.random.uniform(ks[2], (DIM_V, DIM_Q), jnp.float32, -s_in, s_in), 'bq': jax.random.uniform(ks[3], (DIM_V,), jnp.float32, -s_in, s_in), 'Wk': jax.random.uniform(ks[4], (DIM_V, DIM_Q), jnp.float32, -s_in, s_in), 'bk': jax.random.uniform(ks[5], (DIM_V,), jnp.float32, -s_in, s_in), 'Wv': jax.random.uniform(ks[6], (DIM_V, DIM_Q), jnp.float32, -s_in, s_in), 'bv': jax.random.uniform(ks[7], (DIM_V,), jnp.float32, -s_in, s_in), 'Wo': jax.random.uniform(ks[8], (DIM_V, DIM_V), jnp.float32, -s_v, s_v), 'bo': jax.random.uniform(ks[9], (DIM_V,), jnp.float32, -s_v, s_v), 'g0': jnp.ones((DIM_V,), jnp.float32), 'b0': jnp.zeros((DIM_V,), jnp.float32), 'g1': jnp.ones((DIM_V,), jnp.float32), 'b1': jnp.zeros((DIM_V,), jnp.float32)}
    _L1_xattn_all = _L1_xattn_setup()
    _L1_xattn_in = {k: v for k, v in _L1_xattn_all.items() if k in ('Wq', 'bq', 'Wk', 'bk', 'Wv', 'bv', 'Wo', 'bo', 'g0', 'b0', 'g1', 'b1')}
    del _L1_xattn_all

    def _L1_ffn_setup():
        import jax, jax.numpy as jnp
        import numpy as np
        TOP_K = 2
        EPS = 1e-09
        key = jax.random.key(seed)
        ks = jax.random.split(key, 6)
        B, T, D, H, E = (4, 512, 256, 512, 8)
        x = jax.random.normal(ks[0], (B, T, D), dtype=jnp.float32)
        Wg = jax.random.normal(ks[1], (E, D), dtype=jnp.float32) * 0.02
        W1 = jax.random.normal(ks[2], (E, 2 * H, D), dtype=jnp.float32) * 0.02
        b1 = jax.random.normal(ks[3], (E, 2 * H), dtype=jnp.float32) * 0.02
        Wo = jax.random.normal(ks[4], (D, H), dtype=jnp.float32) * 0.02
        bo = jax.random.normal(ks[5], (D,), dtype=jnp.float32) * 0.02
        return {'x': x, 'Wg': Wg, 'W1': W1, 'b1': b1, 'Wo': Wo, 'bo': bo}
    _L1_ffn_all = _L1_ffn_setup()
    _L1_ffn_in = {k: v for k, v in _L1_ffn_all.items() if k in ('Wg', 'W1', 'b1', 'Wo', 'bo')}
    del _L1_ffn_all
    return {'x': x, 'ctx_1024': ctx_1024, 'L0_xattn_Wq': _L0_xattn_in['Wq'], 'L0_xattn_bq': _L0_xattn_in['bq'], 'L0_xattn_Wkv': _L0_xattn_in['Wkv'], 'L0_xattn_bkv': _L0_xattn_in['bkv'], 'L0_ffn_centroids': _L0_ffn_in['centroids'], 'L0_ffn_ln_g': _L0_ffn_in['ln_g'], 'L0_ffn_ln_b': _L0_ffn_in['ln_b'], 'L0_ffn_w1': _L0_ffn_in['w1'], 'L0_ffn_b1': _L0_ffn_in['b1'], 'L0_ffn_w2': _L0_ffn_in['w2'], 'L0_ffn_b2': _L0_ffn_in['b2'], 'L1_xattn_Wq': _L1_xattn_in['Wq'], 'L1_xattn_bq': _L1_xattn_in['bq'], 'L1_xattn_Wk': _L1_xattn_in['Wk'], 'L1_xattn_bk': _L1_xattn_in['bk'], 'L1_xattn_Wv': _L1_xattn_in['Wv'], 'L1_xattn_bv': _L1_xattn_in['bv'], 'L1_xattn_Wo': _L1_xattn_in['Wo'], 'L1_xattn_bo': _L1_xattn_in['bo'], 'L1_xattn_g0': _L1_xattn_in['g0'], 'L1_xattn_b0': _L1_xattn_in['b0'], 'L1_xattn_g1': _L1_xattn_in['g1'], 'L1_xattn_b1': _L1_xattn_in['b1'], 'L1_ffn_Wg': _L1_ffn_in['Wg'], 'L1_ffn_W1': _L1_ffn_in['W1'], 'L1_ffn_b1': _L1_ffn_in['b1'], 'L1_ffn_Wo': _L1_ffn_in['Wo'], 'L1_ffn_bo': _L1_ffn_in['bo']}

def reference(x, ctx_1024, L0_xattn_Wq, L0_xattn_bq, L0_xattn_Wkv, L0_xattn_bkv, L0_ffn_centroids, L0_ffn_ln_g, L0_ffn_ln_b, L0_ffn_w1, L0_ffn_b1, L0_ffn_w2, L0_ffn_b2, L1_xattn_Wq, L1_xattn_bq, L1_xattn_Wk, L1_xattn_bk, L1_xattn_Wv, L1_xattn_bv, L1_xattn_Wo, L1_xattn_bo, L1_xattn_g0, L1_xattn_b0, L1_xattn_g1, L1_xattn_b1, L1_ffn_Wg, L1_ffn_W1, L1_ffn_b1, L1_ffn_Wo, L1_ffn_bo):
    import jax
    import jax.numpy as jnp

    def _L0_xattn_ref(x, text_input, Wq, bq, Wkv, bkv):
        import jax, jax.numpy as jnp
        import numpy as np
        B, LQ, LK, D = (4, 512, 512, 256)
        H = 16
        HD = D // H
        b, lq, d = x.shape
        lk = text_input.shape[1]
        Q = x @ Wq + bq
        KV = text_input @ Wkv + bkv
        K, V = jnp.split(KV, 2, axis=-1)
        Q = Q.reshape(b, lq, H, HD)
        K = K.reshape(b, lk, H, HD)
        V = V.reshape(b, lk, H, HD)
        scale = 1.0 / jnp.sqrt(jnp.asarray(HD, dtype=Q.dtype))
        scores = jnp.einsum('bqhd,bkhd->bhqk', Q, K) * scale
        attn = jax.nn.softmax(scores, axis=-1)
        out = jnp.einsum('bhqk,bkhd->bqhd', attn, V)
        return out.reshape(b, lq, d)

    def _L0_ffn_ref(input_features, centroids, ln_g, ln_b, w1, b1, w2, b2):
        import jax, jax.numpy as jnp
        import numpy as np
        E, D, F = (8, 256, 1024)
        LN_EPS = 1e-05
        x = input_features.reshape(-1, D)
        aff = jax.lax.stop_gradient(x) @ centroids.T
        assign = jnp.argmax(aff, axis=1)
        onehot = jax.nn.one_hot(assign, E, dtype=x.dtype)
        mu = jnp.mean(x, axis=-1, keepdims=True)
        var = jnp.mean((x - mu) ** 2, axis=-1, keepdims=True)
        xhat = (x - mu) * jax.lax.rsqrt(var + LN_EPS)
        xn = xhat[None, :, :] * ln_g[:, None, :] + ln_b[:, None, :]
        h = jax.nn.relu(jnp.einsum('etd,efd->etf', xn, w1) + b1[:, None, :])
        y = x[None, :, :] + jnp.einsum('etf,edf->etd', h, w2) + b2[:, None, :]
        alpha = jax.nn.sigmoid(x @ centroids.T)
        a = alpha.T[:, :, None]
        gated = a * y + (1.0 - a) * x[None, :, :]
        out = jnp.einsum('te,etd->td', onehot, gated)
        return out.reshape(input_features.shape)

    def _L1_xattn_ref(Q, K, Wq, bq, Wk, bk, Wv, bv, Wo, bo, g0, b0, g1, b1):
        import jax, jax.numpy as jnp
        import numpy as np
        DIM_Q = 256
        DIM_V = 256
        NUM_HEADS = 8
        LN_EPS = 1e-05

        def _layernorm(x, gamma, beta):
            mu = jnp.mean(x, axis=-1, keepdims=True)
            var = jnp.mean((x - mu) ** 2, axis=-1, keepdims=True)
            return (x - mu) * jax.lax.rsqrt(var + LN_EPS) * gamma + beta
        B, NQ, _ = Q.shape
        NK = K.shape[1]
        H = NUM_HEADS
        dh = DIM_V // H
        q = Q @ Wq.T + bq
        k = K @ Wk.T + bk
        v = K @ Wv.T + bv
        qh = q.reshape(B, NQ, H, dh)
        kh = k.reshape(B, NK, H, dh)
        vh = v.reshape(B, NK, H, dh)
        scores = jnp.einsum('bqhd,bkhd->bhqk', qh, kh) / np.sqrt(DIM_V).astype(np.float32)
        A = jax.nn.softmax(scores, axis=-1)
        oh = qh + jnp.einsum('bhqk,bkhd->bqhd', A, vh)
        O = oh.reshape(B, NQ, DIM_V)
        O = _layernorm(O, g0, b0)
        O = O + jax.nn.relu(O @ Wo.T + bo)
        O = _layernorm(O, g1, b1)
        return O

    def _L1_ffn_ref(x, Wg, W1, b1, Wo, bo):
        import jax, jax.numpy as jnp
        import numpy as np
        TOP_K = 2
        EPS = 1e-09
        E = Wg.shape[0]
        gate_logits = jnp.einsum('btd,ed->bte', x, Wg)
        gate_scores = jax.nn.softmax(gate_logits, axis=-1)
        topk_val, topk_idx = jax.lax.top_k(gate_scores, TOP_K)
        topk_val = topk_val / (topk_val.sum(axis=-1, keepdims=True) + EPS)
        comb = (jax.nn.one_hot(topk_idx, E, dtype=x.dtype) * topk_val[..., None]).sum(axis=-2)
        out = jnp.zeros_like(x)
        for e in range(E):
            h = jnp.einsum('btd,hd->bth', x, W1[e]) + b1[e]
            a, b = jnp.split(h, 2, axis=-1)
            g = a * jax.nn.sigmoid(b)
            eo = jnp.einsum('bth,dh->btd', g, Wo) + bo
            out = out + eo * comb[..., e:e + 1]
        return out
    x = x + _L0_xattn_ref(_layernorm(x, axis=-1), ctx_1024, L0_xattn_Wq, L0_xattn_bq, L0_xattn_Wkv, L0_xattn_bkv)
    x = x + _L0_ffn_ref(_layernorm(x, axis=-1), L0_ffn_centroids, L0_ffn_ln_g, L0_ffn_ln_b, L0_ffn_w1, L0_ffn_b1, L0_ffn_w2, L0_ffn_b2)
    x = x + _L1_xattn_ref(_layernorm(x, axis=-1), ctx_1024, L1_xattn_Wq, L1_xattn_bq, L1_xattn_Wk, L1_xattn_bk, L1_xattn_Wv, L1_xattn_bv, L1_xattn_Wo, L1_xattn_bo, L1_xattn_g0, L1_xattn_b0, L1_xattn_g1, L1_xattn_b1)
    x = x + _L1_ffn_ref(_layernorm(x, axis=-1), L1_ffn_Wg, L1_ffn_W1, L1_ffn_b1, L1_ffn_Wo, L1_ffn_bo)
    return x

_drawn_inputs = setup_inputs


def setup_inputs(seed=0):
    import zlib

    import numpy as np

    out = dict(_drawn_inputs(seed))
    spreads = {'L0_xattn_bq': (0.0, 0.509),
     'L0_xattn_bkv': (0.0, 0.1),
     'L0_ffn_ln_g': (1.0, 0.2),
     'L0_ffn_ln_b': (0.0, 0.276),
     'L0_ffn_b1': (0.0, 0.274),
     'L0_ffn_b2': (0.0, 0.1),
     'L1_xattn_g0': (1.0, 0.2),
     'L1_xattn_b0': (0.0, 0.1),
     'L1_xattn_g1': (1.0, 0.2),
     'L1_xattn_b1': (0.0, 0.1)}
    factors = {'L0_xattn_Wq': 2.819,
     'L1_xattn_Wk': 6.525,
     'L1_xattn_bk': 64.0,
     'L1_xattn_bo': 5.473,
     'L1_ffn_Wg': 2.957,
     'L1_ffn_b1': 37.882,
     'L1_ffn_bo': 6.379}
    for name, (base, spread) in spreads.items():
        noise = np.random.default_rng([zlib.crc32(name.encode()), seed]).standard_normal(out[name].shape)
        drawn = base * np.exp(spread * noise) if base else spread * noise
        out[name] = jnp.asarray(drawn.astype(out[name].dtype))
    for name, factor in factors.items():
        out[name] = (out[name] * factor).astype(out[name].dtype)
    return out
```

```python
from contextlib import ExitStack

import concourse.bass as bass
from concourse import mybir

ALU = mybir.AluOpType
ACT = mybir.ActivationFunctionType
F32 = mybir.dt.float32
BF16 = mybir.dt.bfloat16
I32 = mybir.dt.int32
AX_X = mybir.AxisListType.X

NB, LQ, LK, D = 32, 100, 361, 256
DC = D // 128
KTILES = [(0, 121), (121, 120), (241, 120)]
E = 8
F = 1024
FC = F // 128
GH = F // 2
TOK = NB * LQ
LN_EPS = 1e-5


def slot_tiles(pairs):
    return (pairs + E * 127) // 128


NT0 = slot_tiles(TOK)
NT1 = slot_tiles(2 * TOK)
NTMAX = 64


class Batch:

    def __init__(self, r, p, low):
        self.r, self.p, self.low = r, p, low

    def count(self, n, c=0):
        return self.r * (2 * n) + (self.p * n + c)

    @property
    def at(self):
        return self.r * 2 + self.p

    def plus(self, k):
        q = self.p + k
        return Batch(self.r + q // 2, q % 2, self.low + k)


def fixed(b):
    return Batch(b // 2, b % 2, b)


LOOP_FROM, LOOP_TO = 2, NB - 4


def run_steps(engine, step):

    def peeled(t):
        step(fixed(t + 2).plus(-2), 0 <= t + 1 < NB, t + 2 < NB, 0 <= t < NB, 0 <= t - 1 < NB)

    for t in range(-1, LOOP_FROM):
        peeled(t)
    with engine.Fori(LOOP_FROM // 2, LOOP_TO // 2) as i:
        for p in range(2):
            step(Batch(i, p, LOOP_FROM + p), True, True, True, True)
    for t in range(LOOP_TO, NB + 1):
        peeled(t)


def stage_semaphore(nc, sems, name):
    sems.append(nc.alloc_semaphore(name=name))
    return sems[-1]


def end_stage(nc, sems):
    nc.clear_and_free_semaphores(sems)
    nc.all_engine_barrier()


class Links:

    def __init__(self, engine, sem):
        self.engine, self.sem, self.base, self.n = engine, sem, 0, 0

    def __call__(self, instruction):
        instruction.then_inc(self.sem, 1)
        self.n += 1
        self.engine.wait_ge(self.sem, self.base + self.n)


def attention(nc, layer, t, env):
    H = 16 if layer == 0 else 8
    HD = D // H
    NH2 = H // 2
    VW = 32 if layer == 0 else 64
    HG = 128 // VW
    NG = H // HG
    NP = H // 2
    SLOTS = [(kt, s) for s in range(H // 8) for kt in range(3)]
    NS = len(SLOTS)
    SCALE = 0.25 if layer == 0 else 1.0 / 16.0
    X = env["X"]
    tag = f"a{layer}_"

    sems = []
    with ExitStack() as ctx:
        def sb(name, shape, dt=F32):
            return ctx.enter_context(nc.sbuf_tensor(tag + name, shape, dt))

        def sem(name):
            return stage_semaphore(nc, sems, tag + name)

        wq = sb("wq", [128, DC, D])
        wk = sb("wk", [128, DC, D])
        wv = sb("wv", [128, DC, D])
        bq = sb("bq", [128, DC])
        bk = sb("bk", [128, DC])
        bvb = sb("bvb", [LQ, D])
        rows = sb("rows", [LQ, E, D])
        ident = sb("ident", [128, 128])
        neg_ident = sb("neg_ident", [LQ, LQ], BF16)
        ones_bf = sb("ones_bf", [LQ, 128], BF16)
        mask = sb("mask", [128, NH2])
        half_neg = sb("half_neg", [LQ, 1])
        ct = [sb(f"ct{p}", [128, DC, LK]) for p in range(2)]
        xh = sb("xh", [LQ, D])
        xT = sb("xT", [128, DC, LQ])
        QM = [sb(f"QM{p}", [128, H, LQ]) for p in range(2)]
        QMb = sb("QMb", [128, H, LQ], BF16)
        KT = [sb(f"KT{p}", [128, DC, LK]) for p in range(2)]
        KTb = sb("KTb", [128, DC, LK], BF16)
        V = [sb(f"V{p}", [128, 3, H, VW]) for p in range(2)]
        mx = sb("mx", [LQ, H])
        DM = sb("DM", [LQ, H, LQ], BF16)
        Pr = sb("Pr", [128, 3, H * LQ])
        avs = sb("avs", [128, NG, LQ])
        rs = sb("rs", [LQ, H])
        o = sb("o", [LQ, D])
        st = sb("st", [LQ, 6])
        NL = 3 if layer == 0 else 4
        mv = [sb(f"mv{k}", [LQ, 2]) for k in range(NL)]
        ve = [sb(f"ve{k}", [LQ, 1]) for k in range(NL)]
        rstd = [sb(f"rstd{k}", [LQ, 1]) for k in range(NL)]
        xp = sb("xp", [LQ, D])
        keep = sb("keep", [LQ, D])
        junk = sb("junk", [LQ, E, D])
        aff = sb("aff", [LQ, E])
        if layer == 1:
            bqb = sb("bqb", [LQ, D])
            wo = sb("wo", [128, DC, D])
            g0b, b0b, g1b, b1b, bob = (sb(n, [LQ, D]) for n in ("g0b", "b0b", "g1b", "b1b", "bob"))
            qtok = [sb(f"qtok{p}", [LQ, D]) for p in range(2)]
            o1 = sb("o1", [LQ, D])
            o2 = sb("o2", [LQ, D])
            oT = sb("oT", [128, DC, LQ])
            yg = [sb(f"yg{p}", [LQ, D]) for p in range(2)]
            gidx = [sb(f"gidx{p}", [LQ, 1], I32) for p in range(2)]

        ST = ctx.enter_context(nc.psum_tensor(tag + "ST", [128, 2, 2, 512], F32))
        SM = ctx.enter_context(nc.psum_tensor(tag + "SM", [128, 2, 512], F32))
        M0 = ctx.enter_context(nc.psum_tensor(tag + "M0", [128, 512], F32))
        M1 = ctx.enter_context(nc.psum_tensor(tag + "M1", [128, 512], F32))

        loaded = sem("loaded")
        x_loaded = sem("x_loaded")
        ct_loaded = [sem(f"ct_loaded{p}") for p in range(2)]
        pads_set = sem("pads_set")
        xh_ready = sem("xh_ready")
        xT_ps = sem("xT_ps")
        xT_sb = sem("xT_sb")
        q_ps = sem("q_ps")
        k_ps = sem("k_ps")
        v_ps = sem("v_ps")
        qm_ready = sem("qm_ready")
        qmb_ready = sem("qmb_ready")
        k_evac = sem("k_evac")
        ktb_ready = sem("ktb_ready")
        v_evac = sem("v_evac")
        qtok_ready = sem("qtok_ready")
        qtok_used = sem("qtok_used")
        sm_ps = sem("sm_ps")
        max_done = sem("max_done")
        dm_ready = sem("dm_ready")
        st_ps = sem("st_ps")
        exp_done = sem("exp_done")
        av_ps = sem("av_ps")
        avs_copied = sem("avs_copied")
        avt_ps = sem("avt_ps")
        norm_read = sem("norm_read")
        var_ready = [sem(f"var_ready{k}") for k in range(NL)]
        rstd_ready = [sem(f"rstd_ready{k}") for k in range(NL)]
        keep_ready = sem("keep_ready")
        keep_stored = sem("keep_stored")
        w1_loaded = sem("w1_loaded")
        dve_own = [sem(f"dve_own{k}") for k in range(3)]
        dve_turns = sem("dve_turns")
        pool_turns = env["pool_turns"]
        o1_ready = sem("o1_ready")
        oT_ps = sem("oT_ps")
        oT_sb = sem("oT_sb")
        wo_ps = sem("wo_ps")
        wo_used = sem("wo_used")
        yg_loaded = [sem(f"yg_loaded{p}") for p in range(2)]
        x2_done = sem("x2_done")
        gidx_ready = sem("gidx_ready")

        small = [(wq, t["wq"]), (wk, t["wk"]), (wv, t["wv"]), (bq, t["bq"]), (bk, t["bk"]),
                 (bvb, t["bv"].partition_broadcast(LQ)), (rows, t["rows"].partition_broadcast(LQ)),
                 (ident, t["ident"]), (mask, t["mask"])]
        if layer == 1:
            small += [(wo, t["wo"]), (bqb, t["bq_row"].partition_broadcast(LQ))]
            small += [(w, t[n].partition_broadcast(LQ))
                      for w, n in ((g0b, "g0"), (b0b, "b0"), (g1b, "g1"), (b1b, "b1"), (bob, "bo"))]
        ALL_LOADED = 16 * len(small)

        block = ctx.enter_context(nc.Block())

        @block.sync
        def _(sp):
            def load(b):
                if b.low >= 2:
                    sp.wait_ge(v_ps, b.count(2, -2))
                sp.dma_start(ct[b.p][:], t["ctx"][bass.ds(b.at, 1)].rearrange("o p c k -> p (o c) k")
                             ).then_inc(ct_loaded[b.p], 16)

            def store(b):
                sp.wait_ge(keep_ready, b.count(1, 1))
                sp.dma_start(t["keep"][bass.ds(b.at * LQ, LQ), :], keep[:]).then_inc(keep_stored, 16)

            if layer == 0:
                sp.dma_start(X[:, 0:4], t["x"][0:4].rearrange("b q d -> q b d")).then_inc(x_loaded, 16)
            for dst, src in small:
                sp.dma_start(dst[:], src).then_inc(loaded, 16)
            load(fixed(0))
            load(fixed(1))
            if layer == 0:
                sp.dma_start(X[:, 4:NB], t["x"][4:NB].rearrange("b q d -> q b d")).then_inc(x_loaded, 16)
            for b in range(2, 4):
                load(fixed(b))
            with sp.Fori(0, E) as i:
                for p in range(2):
                    load(Batch(i + 2, p, 4 + p))
                    store(Batch(i, p, p))
                sp.dma_start(env["w1"][:, bass.ds(i, 1)].rearrange("p o c f -> p (o c f)"),
                             t["w1"][:, bass.ds(i, 1)].rearrange("p o c f -> p (o c f)")).then_inc(w1_loaded, 16)
            with sp.Fori(E, (NB - 4) // 2) as i:
                for p in range(2):
                    load(Batch(i + 2, p, 4 + p))
                    store(Batch(i, p, p))
            for b in range(NB - 4, NB):
                store(fixed(b))
            sp.wait_ge(keep_stored, 16 * NB)
            sp.wait_ge(w1_loaded, 16 * E)

        @block.tensor
        def _(pe):
            def project_k(b, h):
                for c in range(DC):
                    last = nc.tensor.matmul(M1[:, 0:LK], wk[:, c, h * 128:(h + 1) * 128], ct[b.p][:, c, :],
                                            start=(c == 0), stop=(c == DC - 1))
                last.then_inc(k_ps, 1)

            def project_v(b, kt, M, c0):
                k0, n = KTILES[kt]
                for c in range(DC):
                    last = nc.tensor.matmul(M[0:n, c0:c0 + D], ct[b.p][:, c, k0:k0 + n], wv[:, c, :],
                                            start=(c == 0), stop=(c == DC - 1))
                return last

            def first_k(b):
                pe.wait_ge(ct_loaded[b.p], b.r * 16 + 16)
                project_k(b, 0)

            def front(b):
                pe.wait_ge(xh_ready, b.count(1, 1))
                if b.low == 1:
                    pe.wait_ge(v_evac, 2)
                    if layer == 1:
                        pe.wait_ge(qtok_ready, 1)
                for c in range(DC):
                    last = nc.tensor.transpose(M0[:, c * LQ:(c + 1) * LQ], xh[:, c * 128:(c + 1) * 128],
                                               ident[0:LQ, 0:LQ])
                last.then_inc(xT_ps, 1)
                pe.wait_ge(k_evac, b.count(2, 1))
                project_k(b, 1)
                pe.wait_ge(xT_sb, b.count(1, 1))
                for h in range(DC):
                    for c in range(DC):
                        last = nc.tensor.matmul(M0[:, h * LQ:(h + 1) * LQ], wq[:, c, h * 128:(h + 1) * 128],
                                                xT[:, c, :], start=(c == 0), stop=(c == DC - 1))
                last.then_inc(q_ps, 1)
                pe.wait_ge(k_evac, b.count(2, 2))
                project_v(b, 1, M1, 0)
                project_v(b, 2, M1, D).then_inc(v_ps, 1)
                pe.wait_ge(qm_ready, b.count(1, 1))
                last = project_v(b, 0, M0, 0)
                if layer == 1:
                    for c in range(DC):
                        last = nc.tensor.matmul(M0[0:LQ, D:2 * D], xT[:, c, :], wq[:, c, :],
                                                start=(c == 0), stop=(c == DC - 1))
                last.then_inc(v_ps, 1)

            def score_rows(b, j):
                if j == 0:
                    pe.wait_ge(qmb_ready, b.count(1, 1))
                    pe.wait_ge(ktb_ready, b.count(2, 2))
                pe.wait_ge(max_done, b.count(NP, j))
                for h in (2 * j, 2 * j + 1):
                    last = nc.tensor.matmul(SM[0:LQ, h % 2, 0:LK], QMb[:, h, :], KTb[:, h // NH2, :],
                                            start=True, stop=True)
                last.then_inc(sm_ps, 1)

            def scores(b, s):
                kt, eight = SLOTS[s]
                k0, n = KTILES[kt]
                buf = (b.p * NS + s) % 2
                if s == 0:
                    pe.wait_ge(dm_ready, b.count(1, 1))
                    if b.low >= 1:
                        pe.wait_ge(norm_read, b.count(1))
                if b.low >= 1 or s >= 2:
                    pe.wait_ge(exp_done, b.count(NS, s - 1))
                for j in range(2):
                    h = 8 * eight + 4 * j
                    nc.tensor.matmul(ST[0:n, buf, j, 0:4 * LQ], KT[b.p][:, h // NH2, k0:k0 + n],
                                     QM[b.p][:, h:h + 4, :], start=True, stop=False)
                    last = nc.tensor.matmul(ST[0:n, buf, j, 0:4 * LQ], ones_bf[:, 0:n],
                                            DM[:, h:h + 4, :], start=False, stop=True)
                last.then_inc(st_ps, 1)

            def values(b, g):
                for kt in range(3):
                    n = KTILES[kt][1]
                    for j in range(HG):
                        h = g * HG + j
                        last = nc.tensor.matmul(M0[VW * j:VW * (j + 1), g * LQ:(g + 1) * LQ],
                                                V[b.p][0:n, kt, h, :], Pr[0:n, kt, h * LQ:(h + 1) * LQ],
                                                start=(kt == 0), stop=(kt == 2))
                return last

            def out_transposes(b):
                pe.wait_ge(o1_ready, b.count(1, 1))
                for c in range(DC):
                    last = nc.tensor.transpose(M1[:, c * LQ:(c + 1) * LQ], o1[:, c * 128:(c + 1) * 128],
                                               ident[0:LQ, 0:LQ])
                last.then_inc(oT_ps, 1)

            def out_product(b):
                pe.wait_ge(oT_sb, b.count(1, 1))
                for c in range(DC):
                    last = nc.tensor.matmul(M1[0:LQ, 0:D], oT[:, c, :], wo[:, c, :],
                                            start=(c == 0), stop=(c == DC - 1))
                last.then_inc(wo_ps, 1)

            def free_m0(nxt, fr):
                if fr:
                    pe.wait_ge(v_evac, nxt.count(2, 2))
                    if layer == 1:
                        pe.wait_ge(qtok_ready, nxt.count(1, 1))

            def start_k(nxt, nxt2, prev, tail):
                pe.wait_ge(v_evac, nxt.count(2, 1))
                if layer == 1 and tail:
                    pe.wait_ge(wo_used, prev.count(1, 1))
                first_k(nxt2)

            EARLY = 1 if layer == 0 else 0
            EARLY_EXPS = 2 if layer == 0 else 0

            def step(b, fr, ahead, back, tail):
                nxt, nxt2, prev = b.plus(1), b.plus(2), b.plus(-1)
                if fr:
                    front(nxt)
                pair = 0
                for s in range(NS):
                    if back:
                        if s == 4:
                            pe.wait_ge(exp_done, b.count(NS, 3))
                            free_m0(nxt, fr)
                            values(b, 0)
                        scores(b, s)
                    if layer == 1 and tail and s == 2:
                        out_product(prev)
                    if fr:
                        score_rows(nxt, pair)
                        pair += 1
                    if layer == 1 and tail and s == 1:
                        if fr:
                            pe.wait_ge(v_evac, nxt.count(2, 1))
                        out_transposes(prev)
                if layer == 1:
                    if ahead:
                        start_k(nxt, nxt2, prev, tail)
                    if fr:
                        score_rows(nxt, 3)
                for g in range(EARLY, NG):
                    if back:
                        if g == max(EARLY, EARLY_EXPS):
                            pe.wait_ge(exp_done, b.count(NS, NS))
                        if g == 0:
                            free_m0(nxt, fr)
                        last = values(b, g)
                    if fr and layer == 0 and g == 1:
                        score_rows(nxt, 6)
                if back:
                    last.then_inc(av_ps, 1)
                if layer == 0:
                    if ahead:
                        start_k(nxt, nxt2, prev, tail)
                    if fr:
                        score_rows(nxt, 7)
                if back:
                    pe.wait_ge(avs_copied, b.count(1, 1))
                    for g in range(NG):
                        last = nc.tensor.transpose(ST[0:LQ, 0, 0, g * 128:(g + 1) * 128], avs[:, g, :], ident[:])
                    last.then_inc(avt_ps, 1)

            pe.wait_ge(loaded, ALL_LOADED)
            pe.wait_ge(pads_set, 4)
            first_k(fixed(0))
            run_steps(pe, step)

        @block.scalar
        def _(act):
            def copy_k(b, h):
                if b.low >= 2:
                    act.wait_ge(st_ps, b.count(NS, -NS))
                act.wait_ge(k_ps, b.count(2, h + 1))
                nc.scalar.activation(KT[b.p][:, h, :], M1[:, 0:LK], ACT.Identity, bias=bk[:, h:h + 1]
                                     ).then_inc(k_evac, 1)

            def round_k(b, h):
                act.wait_ge(sm_ps, b.count(NP))
                act.wait_ge(k_evac, b.count(2, h + 1))
                nc.scalar.activation(KTb[:, h, :], KT[b.p][:, h, :], ACT.Copy).then_inc(ktb_ready, 1)

            def copy_v(b, kt, M, c0):
                n = KTILES[kt][1]
                return nc.scalar.activation(V[b.p][0:n, kt, :, 0:HD],
                                            M[0:n, c0:c0 + D].rearrange("p (h d) -> p h d", h=H), ACT.Copy)

            def front(b):
                act.wait_ge(v_ps, b.count(2))
                act.wait_ge(xT_ps, b.count(1, 1))
                nc.scalar.activation(xT[:], M0[:, 0:DC * LQ].rearrange("p (c q) -> p c q", c=DC), ACT.Copy
                                     ).then_inc(xT_sb, 1)
                round_k(b, 0)
                copy_k(b, 1)
                round_k(b, 1)
                act.wait_ge(qm_ready, b.count(1, 1))
                nc.scalar.activation(QMb[:], QM[b.p][:], ACT.Copy).then_inc(qmb_ready, 1)
                if b.low >= 2:
                    act.wait_ge(av_ps, b.count(1, -1))
                act.wait_ge(v_ps, b.count(2, 1))
                copy_v(b, 1, M1, 0)
                copy_v(b, 2, M1, D).then_inc(v_evac, 1)
                act.wait_ge(v_ps, b.count(2, 2))
                copy_v(b, 0, M0, 0).then_inc(v_evac, 1)
                if layer == 1:
                    if b.low >= 2:
                        act.wait_ge(qtok_used, b.count(1, -1))
                    nc.scalar.activation(qtok[b.p][:], M0[0:LQ, D:2 * D], ACT.Copy).then_inc(qtok_ready, 1)

            def step(b, fr, ahead, back, tail):
                if fr:
                    front(b.plus(1))
                if back:
                    act.wait_ge(av_ps, b.count(1))
                for s, (kt, eight) in enumerate(SLOTS):
                    if back:
                        n = KTILES[kt][1]
                        act.wait_ge(st_ps, b.count(NS, s + 1))
                        dst = Pr[0:n, kt, eight * 8 * LQ:(eight + 1) * 8 * LQ]
                        nc.scalar.activation(dst.rearrange("p (j q) -> p j q", j=2),
                                             ST[0:n, (b.p * NS + s) % 2, :, 0:4 * LQ], ACT.Exp, scale=SCALE
                                             ).then_inc(exp_done, 1)
                    if layer == 1 and tail and s == 1:
                        prev = b.plus(-1)
                        act.wait_ge(oT_ps, prev.count(1, 1))
                        act.wait_ge(wo_ps, prev.count(1))
                        nc.scalar.activation(oT[:], M1[:, 0:DC * LQ].rearrange("p (c q) -> p c q", c=DC),
                                             ACT.Copy).then_inc(oT_sb, 1)
                if back:
                    act.wait_ge(av_ps, b.count(1, 1))
                    act.wait_ge(avt_ps, b.count(1))
                    nc.scalar.activation(avs[:], M0[:, 0:NG * LQ].rearrange("p (g q) -> p g q", g=NG), ACT.Copy
                                         ).then_inc(avs_copied, 1)
                if ahead:
                    copy_k(b.plus(2), 0)

            act.wait_ge(loaded, ALL_LOADED)
            act.wait_ge(pads_set, 4)
            copy_k(fixed(0), 0)
            run_steps(act, step)

        @block.gpsimd
        def _(pool):
            def wait_apart():
                pool.sem_inc(pool_turns, 1)

            def power(k, b):
                pool.wait_ge(var_ready[k], b.count(1, 1))
                nc.gpsimd.tensor_tensor(rstd[k][:], ve[k][:], half_neg[:], ALU.pow).then_inc(rstd_ready[k], 1)

            def gather(b):
                if b.low >= 2:
                    pool.wait_ge(x2_done, b.count(1, -1))
                wait_apart()
                nc.gpsimd.tensor_copy(gidx[b.p][:], env["slots"][:, bass.ds(b.at, 1)]).then_inc(gidx_ready, 1)
                pool.wait_ge(gidx_ready, b.count(1, 1))
                wait_apart()
                nc.gpsimd.indirect_dma_start(yg[b.p][:], None, t["ys"], bass.IndirectOffsetOnAxis(gidx[b.p][:], 0)
                                             ).then_inc(yg_loaded[b.p], 16)

            def diagonals(b):
                pool.wait_ge(max_done, b.count(NP, NP))
                pool.wait_ge(st_ps, b.count(NS))
                nc.gpsimd.tensor_tensor(DM[:], neg_ident[:].unsqueeze(1).to_broadcast([LQ, H, LQ]),
                                        mx[:].unsqueeze(2).to_broadcast([LQ, H, LQ]), ALU.mult
                                        ).then_inc(dm_ready, 1)

            def step(b, fr, ahead, back, tail):
                nxt, nxt2, prev = b.plus(1), b.plus(2), b.plus(-1)
                if tail:
                    power(1, prev)
                if ahead:
                    if layer == 1 and tail and prev.low >= 1:
                        power(3, prev.plus(-1))
                    power(0, nxt2)
                if layer == 0:
                    if tail:
                        power(2, prev)
                    if fr:
                        diagonals(nxt)
                else:
                    if not ahead and tail:
                        power(3, prev.plus(-1))
                    if fr:
                        diagonals(nxt)
                    if tail:
                        power(2, prev)
                    if ahead and nxt2.low + 1 < NB:
                        gather(nxt2.plus(1))

            nc.gpsimd.memset(half_neg[:], -0.5)
            nc.gpsimd.memset(ones_bf[:], 1.0).then_inc(pads_set, 1)
            for p in range(2):
                nc.gpsimd.memset(V[p][:], 0.0).then_inc(pads_set, 1)
            pool.wait_ge(loaded, ALL_LOADED)
            pool.wait_ge(pads_set, 3)
            for p in range(2):
                nc.gpsimd.memset(V[p][:, :, :, HD:HD + 1], 1.0)
            nc.gpsimd.tensor_scalar(neg_ident[:], ident[0:LQ, 0:LQ], -1.0, 0.0, ALU.mult, ALU.add
                                    ).then_inc(pads_set, 1)
            pool.wait_ge(pads_set, 4)
            if layer == 1:
                gather(fixed(0))
                gather(fixed(1))
            power(0, fixed(0))
            run_steps(pool, step)
            if layer == 1:
                power(3, fixed(NB - 1))

        @block.vector
        def _(dve):
            V_ = nc.vector
            link = Links(dve, dve_own[0])

            def wait_apart():
                dve.sem_inc(dve_turns, 1)

            def norm_stats(k, b, src):
                wait_apart()
                link(V_.bn_stats(st[:], src))
                wait_apart()
                link(V_.bn_aggr(mv[k][:], st[:]))
                V_.tensor_scalar(ve[k][:], mv[k][:, 1:2], LN_EPS, None, ALU.add).then_inc(var_ready[k], 1)

            def rstd_of(k, b):
                dve.wait_ge(rstd_ready[k], b.count(1, 1))

            def normed(out, k, src):
                return V_.tensor_scalar(out, src, mv[k][:, 0:1], rstd[k][:], ALU.subtract, ALU.mult)

            def xrow(b):
                return X[:, bass.ds(b.at, 1), :].rearrange("q o d -> q (o d)")

            def input_stats(b):
                if layer == 1:
                    dve.wait_ge(yg_loaded[b.p], b.r * 16 + 16)
                    V_.scalar_tensor_tensor(xrow(b), yg[b.p][:], env["alpha"][:, bass.ds(b.at, 1)], xrow(b),
                                            ALU.mult, ALU.add).then_inc(x2_done, 1)
                    dve.wait_ge(x2_done, b.count(1, 1))
                norm_stats(0, b, xrow(b))

            def input_rows(b):
                rstd_of(0, b)
                dve.wait_ge(xT_ps, b.count(1))
                normed(xh[:], 0, xrow(b)).then_inc(xh_ready, 1)

            def masked_queries(b):
                dve.wait_ge(q_ps, b.count(1, 1))
                if b.low >= 2:
                    dve.wait_ge(st_ps, b.count(NS, -NS))
                    dve.wait_ge(qmb_ready, b.count(1, -1))
                for h in range(DC):
                    last = V_.scalar_tensor_tensor(
                        QM[b.p][:, h * NH2:(h + 1) * NH2, :],
                        M0[:, h * LQ:(h + 1) * LQ].unsqueeze(1).to_broadcast([128, NH2, LQ]),
                        bq[:, h:h + 1], mask[:].unsqueeze(2).to_broadcast([128, NH2, LQ]), ALU.add, ALU.mult)
                last.then_inc(qm_ready, 1)

            def maxima(b, j):
                if j == 0:
                    dve.wait_ge(dm_ready, b.count(1))
                dve.wait_ge(sm_ps, b.count(NP, j + 1))
                V_.tensor_reduce(mx[:, 2 * j:2 * j + 2], SM[0:LQ, :, 0:LK], AX_X, ALU.max
                                 ).then_inc(max_done, 1)

            def normalise(b):
                dve.wait_ge(avt_ps, b.count(1, 1))
                mm = ST[0:LQ, 0, 0, :].rearrange("q (h w) -> q h w", h=H)
                link(V_.reciprocal(rs[:], mm[:, :, HD]))
                V_.tensor_tensor(o[:].rearrange("q (h d) -> q h d", h=H), mm[:, :, 0:HD],
                                 rs[:].unsqueeze(2).to_broadcast([LQ, H, HD]), ALU.mult).then_inc(norm_read, 1)

            def residual(b):
                dve.wait_ge(norm_read, b.count(1, 1))
                if layer == 0:
                    link(V_.tensor_tensor(o[:], o[:], bvb[:], ALU.add))
                    link(V_.tensor_tensor(xrow(b), xrow(b), o[:], ALU.add))
                else:
                    dve.wait_ge(qtok_ready, b.count(1, 1))
                    V_.tensor_tensor(o[:], o[:], qtok[b.p][:], ALU.add).then_inc(qtok_used, 1)
                    dve.wait_ge(qtok_used, b.count(1, 1))
                    link(V_.tensor_tensor(o[:], o[:], bqb[:], ALU.add))
                norm_stats(1, b, xrow(b) if layer == 0 else o[:])

            def router(b, src, e0, e1):
                for e in range(e0, e1):
                    ins = V_.tensor_tensor_reduce(out=junk[:, e, :], in0=src, in1=rows[:, e, :], scale=1.0,
                                                  scalar=0.0, op0=ALU.mult, op1=ALU.add,
                                                  accum_out=aff[:, e:e + 1])
                link(ins)
                if e1 == E:
                    link(V_.tensor_copy(env["aff"][:, bass.ds(b.at, 1), :].rearrange("q o e -> q (o e)"), aff[:]))

            def kept(b, k, src):
                rstd_of(k, b)
                dve.wait_ge(keep_stored, b.count(16))
                normed(keep[:], k, src).then_inc(keep_ready, 1)

            def tail0(b, j):
                if j == 1:
                    rstd_of(1, b)
                    link(normed(xp[:], 1, xrow(b)))
                    norm_stats(2, b, xp[:])
                elif j == 2:
                    kept(b, 2, xp[:])
                    link(V_.tensor_tensor(xrow(b), xrow(b), xp[:], ALU.add))
                    router(b, xp[:], 0, 2)
                elif j == 3:
                    router(b, xp[:], 2, 6)
                elif j == 4:
                    router(b, xp[:], 6, E)

            def tail1a(b):
                rstd_of(1, b)
                dve.wait_ge(oT_ps, b.count(1))
                link(normed(o1[:], 1, o[:]))
                link(V_.tensor_tensor(o1[:], o1[:], g0b[:], ALU.mult))
                V_.tensor_tensor(o1[:], o1[:], b0b[:], ALU.add).then_inc(o1_ready, 1)
                dve.wait_ge(o1_ready, b.count(1, 1))

            def tail1b(b, j):
                if j == 3:
                    link(V_.scalar_tensor_tensor(o2[:], o2[:], 0.0, o1[:], ALU.max, ALU.add))
                    norm_stats(2, b, o2[:])

            def take_product(b):
                dve.wait_ge(wo_ps, b.count(1, 1))
                V_.tensor_tensor(o2[:], M1[0:LQ, 0:D], bob[:], ALU.add).then_inc(wo_used, 1)
                dve.wait_ge(wo_used, b.count(1, 1))

            def end1a(b):
                rstd_of(2, b)
                link(normed(o2[:], 2, o2[:]))
                link(V_.tensor_tensor(o2[:], o2[:], g1b[:], ALU.mult))

            def end1(b, j):
                if j == 0:
                    link(V_.tensor_tensor(o2[:], o2[:], b1b[:], ALU.add))
                    link(V_.tensor_tensor(xrow(b), xrow(b), o2[:], ALU.add))
                    norm_stats(3, b, xrow(b))
                elif j == 1:
                    kept(b, 3, xrow(b))
                    dve.wait_ge(keep_ready, b.count(1, 1))
                elif j == 3:
                    router(b, keep[:], 0, E)

            def step(b, fr, ahead, back, tail):
                nxt, nxt2, prev = b.plus(1), b.plus(2), b.plus(-1)
                if fr:
                    masked_queries(nxt)
                if tail:
                    residual(prev)
                if tail and layer == 1:
                    if prev.low >= 1:
                        end1a(prev.plus(-1))
                    tail1a(prev)
                for j in range(NP):
                    if layer == 1 and tail and j == 2:
                        take_product(prev)
                    if fr:
                        maxima(nxt, j)
                    if tail:
                        (tail0 if layer == 0 else tail1b)(prev, j)
                    if ahead and j == (0 if layer == 0 else 1):
                        input_stats(nxt2)
                    if ahead and j == (5 if layer == 0 else 2):
                        input_rows(nxt2)
                    if layer == 1 and tail and prev.low >= 1:
                        end1(prev.plus(-1), j)
                if back:
                    normalise(b)

            dve.wait_ge(loaded, ALL_LOADED)
            if layer == 0:
                dve.wait_ge(x_loaded, 32)
            else:
                link(V_.tensor_tensor(bqb[:], bqb[:], bvb[:], ALU.add))
            input_stats(fixed(0))
            input_rows(fixed(0))
            run_dve(dve, step, link, dve_own, OWN_PER_ROUND[layer])
            if layer == 1:
                end1a(fixed(NB - 1))
                for j in range(NP):
                    end1(fixed(NB - 1), j)

    end_stage(nc, sems)


def run_dve(dve, step, link, own, per):
    def peeled(t):
        step(fixed(t + 2).plus(-2), 0 <= t + 1 < NB, t + 2 < NB, 0 <= t < NB, 0 <= t - 1 < NB)

    for t in range(-1, LOOP_FROM):
        peeled(t)
    with dve.Fori(LOOP_FROM // 2, LOOP_TO // 2) as i:
        link.sem, link.base, link.n = own[1], (i - LOOP_FROM // 2) * per, 0
        for p in range(2):
            step(Batch(i, p, LOOP_FROM + p), True, True, True, True)
        assert link.n == per, link.n
    link.sem, link.base, link.n = own[2], 0, 0
    for t in range(LOOP_TO, NB + 1):
        peeled(t)


OWN_PER_ROUND = (30, 38)


def routing(nc, layer, t, env):
    NT = (NT0, NT1)[layer]
    tag = f"r{layer}_"
    BE = NB * E
    sems = []
    with ExitStack() as ctx:
        def sb(name, shape, dt=F32):
            return ctx.enter_context(nc.sbuf_tensor(tag + name, shape, dt))

        def sem(name):
            return stage_semaphore(nc, sems, tag + name)

        before = sb("before", [LQ, LQ])
        ones = sb("ones", [LQ, 128])
        onesr = sb("onesr", [128, NB])
        pref = sb("pref", [128, E])
        starts = sb("starts", [128, NTMAX])
        tile_no = sb("tile_no", [128, NTMAX])
        top = sb("top", [LQ, NB])
        w = sb("w", [LQ, NB, E])
        pr = sb("pr", [LQ, NB, E])
        M = [sb(f"M{k}", [LQ, NB, E]) for k in range(2)]
        MM = sb("MM", [LQ, NB, E])
        pos = sb("pos", [LQ, NB, E])
        tot = sb("tot", [128, NB, E])
        upto = sb("upto", [128, NB, E])
        cmp_ = sb("cmp", [128, E, NTMAX])
        cmp2 = sb("cmp2", [128, NTMAX, E])
        ntile = sb("ntile", [128, E])
        tend = sb("tend", [128, E])
        tbase = sb("tbase", [128, E])
        fl = sb("fl", [128, NTMAX])
        val = [sb(f"val{k}", [LQ, NB]) for k in range(2)]
        den = sb("den", [LQ, NB])
        tile_i = sb("tile_i", [LQ, NB], I32)
        row_i = sb("row_i", [LQ, NB], I32)
        row_no = sb("row_no", [LQ, 128])
        seq_no = sb("seq_no", [LQ, NB])
        tok_no = sb("tok_no", [LQ, 1])
        in_row = [sb(f"in_row{k}", [LQ, NB, 128], BF16) for k in range(layer + 1)]
        in_tile = [sb(f"in_tile{k}", [LQ, NB, 2, NT], BF16) for k in range(layer + 1)]
        tok_f = sb("tok_f", [128, NT])
        PS = ctx.enter_context(nc.psum_tensor(tag + "PS", [128, 3, 512], F32))

        loaded = sem("loaded")
        own = sem("own")
        act_ready = sem("act_ready")
        act_done = sem("act_done")
        mask_ready = sem("mask_ready")
        counted = sem("counted")
        slots_ready = sem("slots_ready")
        listed = sem("listed")
        consts = [(before, t["before"]), (pref, t["pref"]), (starts, t["starts"]), (tile_no, t["tile_no"]),
                  (row_no, t["row_no"]), (seq_no, t["seq_no"]), (tok_no, t["tok_no"])]
        block = ctx.enter_context(nc.Block())
        AFF = env["aff"]

        @block.sync
        def _(sp):
            for dst, src in consts:
                sp.dma_start(dst[:], src).then_inc(loaded, 16)
            for dst, src in env["second"]:
                sp.dma_start(dst, src).then_inc(env["second_loaded"], 16)

        @block.scalar
        def _(act):
            act.wait_ge(act_ready, 1)
            if layer == 0:
                nc.scalar.activation(env["alpha"][:], top[:], ACT.Sigmoid).then_inc(act_done, 1)
            else:
                nc.scalar.activation(pr[:], w[:], ACT.Exp).then_inc(act_done, 1)

        @block.tensor
        def _(pe):
            pe.wait_ge(mask_ready, 1)
            nc.tensor.matmul(PS[0:LQ, 0, 0:BE], before[:], MM[:].rearrange("q b e -> q (b e)"),
                             start=True, stop=True)
            nc.tensor.matmul(PS[:, 1, 0:BE], ones[:], MM[:].rearrange("q b e -> q (b e)"),
                             start=True, stop=True).then_inc(counted, 1)
            for k in range(layer + 1):
                pe.wait_ge(slots_ready, k + 1)
                for b in range(NB):
                    last = nc.tensor.matmul(PS[:, 2, 0:2 * NT], in_row[k][:, b, :],
                                            in_tile[k][:, b].rearrange("q a j -> q (a j)"),
                                            start=(k == 0 and b == 0), stop=(k == layer and b == NB - 1))
            last.then_inc(listed, 1)

        @block.vector
        def _(dve):
            V_ = nc.vector
            link = Links(dve, own)

            def over_e(x):
                return x[:].unsqueeze(2).to_broadcast([x.shape[0], x.shape[1], E])

            def over_b(x, n):
                return x[0:n, :].unsqueeze(1).to_broadcast([n, NB, E])

            def first_max(k, src):
                link(V_.tensor_reduce(top[:], src, AX_X, ALU.max))
                link(V_.tensor_tensor(w[:], src, over_e(top), ALU.is_equal))
                link(V_.tensor_tensor(w[:], w[:], over_b(pref, LQ), ALU.mult))
                link(V_.tensor_reduce(den[:], w[:], AX_X, ALU.max))
                link(V_.tensor_tensor(M[k][:], w[:], over_e(den), ALU.is_equal))

            dve.wait_ge(loaded, 16 * len(consts))
            link(V_.memset(ones[:], 1.0))
            link(V_.memset(onesr[:], 1.0))
            if layer == 0:
                first_max(0, AFF[:])
                V_.tensor_copy(top[:], top[:]).then_inc(act_ready, 1)
                V_.tensor_copy(MM[:], M[0][:]).then_inc(mask_ready, 1)
            else:
                link(V_.tensor_reduce(top[:], AFF[:], AX_X, ALU.max))
                V_.tensor_tensor(w[:], AFF[:], over_e(top), ALU.subtract).then_inc(act_ready, 1)
                dve.wait_ge(act_done, 1)
                link(V_.tensor_reduce(den[:], pr[:], AX_X, ALU.add))
                link(V_.reciprocal(den[:], den[:]))
                link(V_.tensor_tensor(pr[:], pr[:], over_e(den), ALU.mult))
                first_max(0, pr[:])
                link(V_.tensor_copy(val[0][:], top[:]))
                link(V_.scalar_tensor_tensor(pr[:], M[0][:], -2.0, pr[:], ALU.mult, ALU.add))
                first_max(1, pr[:])
                link(V_.tensor_copy(val[1][:], top[:]))
                link(V_.tensor_tensor(MM[:], M[0][:], M[1][:], ALU.add))
                V_.tensor_tensor(den[:], val[0][:], val[1][:], ALU.add).then_inc(mask_ready, 1)
                dve.wait_ge(mask_ready, 1)
                link(V_.tensor_scalar(den[:], den[:], 1e-9, None, ALU.add))
                link(V_.reciprocal(den[:], den[:]))
                for k in range(2):
                    link(V_.tensor_tensor(env["share"][k][:], val[k][:], den[:], ALU.mult))
            dve.wait_ge(counted, 1)
            link(V_.tensor_copy(tot[:].rearrange("p b e -> p (b e)"), PS[:, 1, 0:BE]))
            for e in range(E):
                link(V_.tensor_tensor_scan(upto[:, :, e], onesr[:], tot[:, :, e], 0.0, ALU.mult, ALU.add))
            link(V_.tensor_tensor(cmp_[:], upto[:, NB - 1, :].unsqueeze(2).to_broadcast([128, E, NTMAX]),
                                  starts[:].unsqueeze(1).to_broadcast([128, E, NTMAX]), ALU.is_gt))
            link(V_.tensor_reduce(ntile[:], cmp_[:], AX_X, ALU.add))
            link(V_.tensor_tensor_scan(tend[:], onesr[:, 0:E], ntile[:], 0.0, ALU.mult, ALU.add))
            link(V_.tensor_tensor(tbase[:], tend[:], ntile[:], ALU.subtract))
            link(V_.tensor_scalar(tbase[:], tbase[:], 128.0, None, ALU.mult))
            link(V_.tensor_tensor(cmp2[:], tile_no[:].unsqueeze(2).to_broadcast([128, NTMAX, E]),
                                  tend[:].unsqueeze(1).to_broadcast([128, NTMAX, E]), ALU.is_ge))
            link(V_.tensor_reduce(fl[:], cmp2[:], AX_X, ALU.add))
            link(V_.tensor_scalar(fl[:], fl[:], float(E - 1), None, ALU.min))
            link(V_.tensor_copy(env["tile_e"][:], fl[:]))
            link(V_.tensor_tensor(upto[:], upto[:], tot[:], ALU.subtract))
            link(V_.tensor_tensor(pos[:].rearrange("q b e -> q (b e)"), PS[0:LQ, 0, 0:BE],
                                  upto[0:LQ].rearrange("q b e -> q (b e)"), ALU.add))
            link(V_.tensor_tensor(pos[:], pos[:], over_b(tbase, LQ), ALU.add))
            for k in range(layer + 1):
                link(V_.tensor_tensor(w[:], pos[:], M[k][:], ALU.mult))
                link(V_.tensor_reduce(den[:], w[:], AX_X, ALU.add))
                link(V_.tensor_copy(env["slots"][k][:], den[:]))
                link(V_.tensor_scalar(tile_i[:], env["slots"][k][:], 7, None, ALU.logical_shift_right))
                link(V_.tensor_scalar(row_i[:], env["slots"][k][:], 127, None, ALU.bitwise_and))
                link(V_.tensor_tensor(in_row[k][:], row_no[:].unsqueeze(1).to_broadcast([LQ, NB, 128]),
                                      row_i[:].unsqueeze(2).to_broadcast([LQ, NB, 128]), ALU.is_equal))
                link(V_.tensor_tensor(in_tile[k][:, :, 1, :],
                                      tile_no[0:LQ, 0:NT].unsqueeze(1).to_broadcast([LQ, NB, NT]),
                                      tile_i[:].unsqueeze(2).to_broadcast([LQ, NB, NT]), ALU.is_equal))
                link(V_.tensor_tensor(in_tile[k][:, :, 0, :], in_tile[k][:, :, 1, :],
                                      seq_no[:].unsqueeze(2).to_broadcast([LQ, NB, NT]), ALU.mult))
                V_.tensor_scalar(in_tile[k][:, :, 1, :], in_tile[k][:, :, 1, :], tok_no[:], None, ALU.mult
                                 ).then_inc(slots_ready, 1)
                dve.wait_ge(slots_ready, k + 1)
            dve.wait_ge(listed, 1)
            link(V_.tensor_copy(tok_f[:], PS[:, 2, NT:2 * NT]))
            link(V_.scalar_tensor_tensor(env["toks"][:, 0:NT], PS[:, 2, 0:NT], float(LQ), tok_f[:],
                                         ALU.mult, ALU.add))
            if layer == 0:
                dve.wait_ge(act_done, 1)

    end_stage(nc, sems)


def expert_tiles(nc, layer, t, env):
    NT = (NT0, NT1)[layer]
    G = FC if layer == 0 else FC // 2
    SECOND = 16 * len(env["second"])
    tag = f"e{layer}_"
    sems = []
    with ExitStack() as ctx:
        def sb(name, shape, dt=F32):
            return ctx.enter_context(nc.sbuf_tensor(tag + name, shape, dt))

        def sem(name):
            return stage_semaphore(nc, sems, tag + name)

        w1 = env["w1"]
        ident = sb("ident", [128, 128])
        if layer == 0:
            w2 = env["second_buf"]
            lng = sb("lng", [128, E * DC])
            lnb = sb("lnb", [128, E * DC])
            b1 = sb("b1", [128, E * FC])
            b2 = sb("b2", [128, E, D])
        else:
            wo = sb("wo", [128, G, D])
            b1 = env["second_buf"]
            b2 = sb("b2", [128, D])
            ab = sb("ab", [128, F])
            sg = sb("sg", [128, GH])
        gidx = sb("gidx", [128, 1], I32)
        xs = sb("xs", [128, D])
        xT = sb("xT", [128, DC, 128])
        hs = sb("hs", [128, F if layer == 0 else GH])
        hT = sb("hT", [128, G, 128])
        y = [sb(f"y{p}", [128, D]) for p in range(2)]
        PX = ctx.enter_context(nc.psum_tensor(tag + "PX", [128, 512], F32))
        PH = ctx.enter_context(nc.psum_tensor(tag + "PH", [128, 2, 512], F32))
        PT = ctx.enter_context(nc.psum_tensor(tag + "PT", [128, 2, 4, 128], F32))
        PY = ctx.enter_context(nc.psum_tensor(tag + "PY", [128, 512], F32))

        small_loaded = sem("small_loaded")
        turns = env["pool_turns"]
        idx_ready = sem("idx_ready")
        rows_loaded = sem("rows_loaded")
        x_ps = sem("x_ps")
        xT_ready = sem("xT_ready")
        h_ps = sem("h_ps")
        h_read = sem("h_read")
        sig_in = sem("sig_in")
        sig_done = sem("sig_done")
        h_ready = sem("h_ready")
        hT_ps = sem("hT_ps")
        hT_act = sem("hT_act")
        hT_dve = sem("hT_dve")
        y_ps = sem("y_ps")
        y_ready = sem("y_ready")
        y_stored = [sem(f"y_stored{p}") for p in range(2)]

        small = [(ident, t["ident"])]
        if layer == 0:
            small += [(lng, t["lng"]), (lnb, t["lnb"]), (b1, t["b1"]), (b2, t["b2"].partition_broadcast(128))]
        else:
            small += [(wo, t["wo"]), (b2, t["b2"].partition_broadcast(128))]
        block = ctx.enter_context(nc.Block())

        @block.sync
        def _(sp):
            for dst, src in small:
                sp.dma_start(dst[:], src).then_inc(small_loaded, 16)

            def store(j, p, r):
                sp.wait_ge(y_ready, j + 1)
                sp.dma_start(t["ys"][bass.ds(j * 128, 128), :], y[p][:]).then_inc(y_stored[p], 16)

            with sp.Fori(0, NT // 2) as i:
                for p in range(2):
                    store(i * 2 + p, p, i)
            if NT % 2:
                store(NT - 1, 0, NT // 2)
            sp.wait_ge(y_stored[0], 16 * ((NT + 1) // 2))
            sp.wait_ge(y_stored[1], 16 * (NT // 2))

        @block.gpsimd
        def _(pool):
            def gather(j, first):
                if not first:
                    pool.wait_ge(x_ps, j)
                pool.sem_inc(turns, 1)
                nc.gpsimd.tensor_copy(gidx[:], env["toks"][:, bass.ds(j, 1)]).then_inc(idx_ready, 1)
                pool.wait_ge(idx_ready, j + 1)
                pool.sem_inc(turns, 1)
                nc.gpsimd.indirect_dma_start(xs[:], None, t["keep"], bass.IndirectOffsetOnAxis(gidx[:], 0)
                                             ).then_inc(rows_loaded, 16)

            gather(0, True)
            with pool.Fori(1, NT) as j:
                gather(j, False)

        def expert_of(engine, j):
            return engine.value_load(env["tile_e"][0:1, bass.ds(j, 1)], min_val=0, max_val=E - 1)

        @block.tensor
        def _(pe):
            def rows(j, first):
                pe.wait_ge(rows_loaded, j * 16 + 16)
                if not first:
                    pe.wait_ge(xT_ready, j)
                for c in range(DC):
                    last = nc.tensor.transpose(PX[:, c * 128:(c + 1) * 128], xs[:, c * 128:(c + 1) * 128], ident[:])
                last.then_inc(x_ps, 1)

            def up(j, first):
                e = expert_of(pe, j)
                pe.wait_ge(xT_ready, j + 1)
                if not first:
                    pe.wait_ge(h_ready if layer == 0 else h_read, j)
                for h in range(2):
                    for c in range(DC):
                        rhs = w1[:, bass.ds(e, 1), c, h * 512:(h + 1) * 512].rearrange("p o f -> p (o f)")
                        last = nc.tensor.matmul(PH[:, h, :], xT[:, c, :], rhs, start=(c == 0), stop=(c == DC - 1))
                last.then_inc(h_ps, 1)

            def turn(j, first):
                pe.wait_ge(h_ready, j + 1)
                if not first:
                    pe.wait_ge(hT_act, j)
                    if layer == 0:
                        pe.wait_ge(hT_dve, j)
                for g in range(G):
                    last = nc.tensor.transpose(PT[:, g // 4, g % 4, :], hs[:, g * 128:(g + 1) * 128], ident[:])
                last.then_inc(hT_ps, 1)

            def down(j, first):
                if layer == 0:
                    e = expert_of(pe, j)
                pe.wait_ge(hT_act, j + 1)
                if layer == 0:
                    pe.wait_ge(hT_dve, j + 1)
                if not first:
                    pe.wait_ge(y_ready, j)
                for g in range(G):
                    rhs = wo[:, g, :] if layer else w2[:, bass.ds(e, 1), g, :].rearrange("p o f -> p (o f)")
                    last = nc.tensor.matmul(PY[:, 0:D], hT[:, g, :], rhs, start=(g == 0), stop=(g == G - 1))
                last.then_inc(y_ps, 1)

            pe.wait_ge(small_loaded, 16 * len(small))
            rows(0, True)
            up(0, True)
            rows(1, False)
            turn(0, True)
            up(1, False)
            rows(2, False)
            if layer == 0:
                pe.wait_ge(env["second_loaded"], SECOND)
            down(0, True)
            with pe.Fori(1, NT - 2) as j:
                turn(j, False)
                up(j + 1, False)
                rows(j + 2, False)
                down(j, False)
            turn(NT - 2, False)
            up(NT - 1, False)
            down(NT - 2, False)
            turn(NT - 1, False)
            down(NT - 1, False)

        @block.scalar
        def _(act):
            def tile(j, first):
                if layer == 0:
                    act.wait_ge(h_ps, j + 1)
                    if not first:
                        act.wait_ge(hT_ps, j)
                    nc.scalar.activation(hs[:, 0:512], PH[:, 0, :], ACT.Copy)
                    nc.scalar.activation(hs[:, 512:F], PH[:, 1, :], ACT.Copy).then_inc(h_ready, 1)
                    e = expert_of(act, j)
                    act.wait_ge(hT_ps, j + 1)
                    if not first:
                        act.wait_ge(y_ps, j)
                    for g in range(4):
                        a = nc.scalar.activation(hT[:, g, :], PT[:, 0, g, :], ACT.Relu,
                                                 bias=b1[:, bass.ds(e * FC + g, 1)])
                    a.then_inc(hT_act, 1)
                else:
                    act.wait_ge(sig_in, j + 1)
                    nc.scalar.activation(sg[:], ab[:, GH:F], ACT.Sigmoid).then_inc(sig_done, 1)
                    act.wait_ge(hT_ps, j + 1)
                    if not first:
                        act.wait_ge(y_ps, j)
                    nc.scalar.activation(hT[:], PT[:, 0], ACT.Copy).then_inc(hT_act, 1)

            act.wait_ge(small_loaded, 16 * len(small))
            tile(0, True)
            with act.Fori(1, NT) as j:
                tile(j, False)

        @block.vector
        def _(dve):
            V_ = nc.vector

            def columns(j, first):
                if layer == 0:
                    e = expert_of(dve, j)
                dve.wait_ge(x_ps, j + 1)
                if not first:
                    dve.wait_ge(h_ps, j)
                if layer == 0:
                    for c in range(DC):
                        a = V_.tensor_scalar(xT[:, c, :], PX[:, c * 128:(c + 1) * 128],
                                             lng[:, bass.ds(e * DC + c, 1)], lnb[:, bass.ds(e * DC + c, 1)],
                                             ALU.mult, ALU.add)
                else:
                    a = V_.tensor_copy(xT[:].rearrange("p c q -> p (c q)"), PX[:, 0:D])
                a.then_inc(xT_ready, 1)

            def hidden(j, first):
                if layer == 0:
                    e = expert_of(dve, j)
                    dve.wait_ge(hT_ps, j + 1)
                    if not first:
                        dve.wait_ge(y_ps, j)
                    for g in range(4, G):
                        a = V_.tensor_scalar(hT[:, g, :], PT[:, 1, g - 4, :], b1[:, bass.ds(e * FC + g, 1)], 0.0,
                                             ALU.add, ALU.max)
                    a.then_inc(hT_dve, 1)
                else:
                    e = expert_of(dve, j)
                    dve.wait_ge(h_ps, j + 1)
                    bias = b1[:, bass.ds(e, 1), :].rearrange("p o f -> p (o f)")
                    if not first:
                        dve.wait_ge(h_ready, j)
                    V_.tensor_tensor(ab[:, GH:F], PH[:, 1, :], bias[:, GH:F], ALU.add).then_inc(sig_in, 1)
                    V_.tensor_tensor(ab[:, 0:GH], PH[:, 0, :], bias[:, 0:GH], ALU.add).then_inc(h_read, 1)
                    dve.wait_ge(h_read, j + 1)
                    dve.wait_ge(sig_done, j + 1)
                    if not first:
                        dve.wait_ge(hT_ps, j)
                    V_.tensor_tensor(hs[:], ab[:, 0:GH], sg[:], ALU.mult).then_inc(h_ready, 1)

            def finish(j, p, r, low):
                if layer == 0:
                    e = expert_of(dve, j)
                dve.wait_ge(y_ps, j + 1)
                if low >= 2:
                    dve.wait_ge(y_stored[p], r * 16)
                row = b2[:, bass.ds(e, 1), :].rearrange("p o f -> p (o f)") if layer == 0 else b2[:]
                V_.tensor_tensor(y[p][:], PY[:, 0:D], row, ALU.add).then_inc(y_ready, 1)

            dve.wait_ge(small_loaded, 16 * len(small))
            if layer == 1:
                dve.wait_ge(env["second_loaded"], SECOND)
            columns(0, True)
            columns(1, False)
            if layer == 0:
                hidden(0, True)
                columns(2, False)
                finish(0, 0, 0, 0)
                hidden(1, False)
                columns(3, False)
                finish(1, 1, 0, 1)
                with dve.Fori(1, (NT - 2) // 2) as i:
                    for p in range(2):
                        j = i * 2 + p
                        hidden(j, False)
                        columns(j + 2, False)
                        finish(j, p, i, 2)
                for j in range(NT - 2 - NT % 2, NT):
                    hidden(j, False)
                    if j + 2 < NT:
                        columns(j + 2, False)
                    finish(j, j % 2, j // 2, 2)
            else:
                hidden(0, True)
                hidden(1, False)
                columns(2, False)
                finish(0, 0, 0, 0)
                hidden(2, False)
                columns(3, False)
                finish(1, 1, 0, 1)
                with dve.Fori(1, (NT - 2) // 2) as i:
                    for p in range(2):
                        j = i * 2 + p
                        hidden(j + 1, False)
                        columns(j + 2, False)
                        finish(j, p, i, 2)
                for j in range(NT - 2 - NT % 2, NT):
                    if j + 1 < NT:
                        hidden(j + 1, False)
                    if j + 2 < NT:
                        columns(j + 2, False)
                    finish(j, j % 2, j // 2, 2)

    end_stage(nc, sems)


def combine(nc, t, env):
    X = env["X"]
    sems = []
    with ExitStack() as ctx:
        idx = [[ctx.enter_context(nc.sbuf_tensor(f"c_idx{k}{p}", [LQ, 1], I32)) for p in range(2)] for k in range(2)]
        yg = [[ctx.enter_context(nc.sbuf_tensor(f"c_yg{k}{p}", [LQ, D], F32)) for p in range(2)] for k in range(2)]

        def sem(name):
            return stage_semaphore(nc, sems, "c_" + name)

        turns = env["pool_turns"]
        staged = sem("staged")
        loaded = [[sem(f"loaded{k}{p}") for p in range(2)] for k in range(2)]
        added = sem("added")
        stored = sem("stored")
        block = ctx.enter_context(nc.Block())

        @block.gpsimd
        def _(pool):
            def gathers(p, r, low):
                if low >= 2:
                    pool.wait_ge(added, r * 4 + (2 * p - 2))
                pool.sem_inc(turns, 1)
                for k in range(2):
                    c = nc.gpsimd.tensor_copy(idx[k][p][:], env["slots"][k][:, bass.ds(r * 2 + p, 1)])
                c.then_inc(staged, 1)
                pool.wait_ge(staged, r * 2 + (p + 1))
                pool.sem_inc(turns, 1)
                for k in range(2):
                    nc.gpsimd.indirect_dma_start(yg[k][p][:], None, t["ys"], bass.IndirectOffsetOnAxis(idx[k][p][:], 0)
                                                 ).then_inc(loaded[k][p], 16)

            gathers(0, 0, 0)
            gathers(1, 0, 1)
            with pool.Fori(1, NB // 2) as i:
                for p in range(2):
                    gathers(p, i, 2)

        @block.vector
        def _(dve):
            with dve.Fori(0, NB // 2) as i:
                for p in range(2):
                    b = i * 2 + p
                    row = X[:, bass.ds(b, 1), :].rearrange("q o d -> q (o d)")
                    for k in range(2):
                        dve.wait_ge(loaded[k][p], i * 16 + 16)
                        nc.vector.scalar_tensor_tensor(row, yg[k][p][:], env["share"][k][:, bass.ds(b, 1)], row,
                                                       ALU.mult, ALU.add).then_inc(added, 1)
                        dve.wait_ge(added, i * 4 + (2 * p + k + 1))

        @block.sync
        def _(sp):
            with sp.Fori(0, NB) as b:
                sp.wait_ge(added, b * 2 + 2)
                sp.dma_start(t["out"][bass.ds(b, 1)].rearrange("o q d -> q (o d)"),
                             X[:, bass.ds(b, 1), :].rearrange("q o d -> q (o d)")).then_inc(stored, 16)
            sp.wait_ge(stored, 16 * NB)

    end_stage(nc, sems)


def program(nc, t):
    t["keep"] = nc.dram_tensor("keep_rows", (TOK, D), F32, kind="Internal").ap()
    with ExitStack() as ctx:
        def sb(name, shape, dt=F32):
            return ctx.enter_context(nc.sbuf_tensor(name, shape, dt))

        X = sb("X", [LQ, NB, D])
        affs = sb("affs", [LQ, NB, E])
        alpha = sb("alpha", [LQ, NB])
        share = [sb(f"share{k}", [LQ, NB]) for k in range(2)]
        slots = [sb(f"slots{k}", [LQ, NB], I32) for k in range(2)]
        toks = sb("toks", [128, NTMAX], I32)
        tile_e = sb("tile_e", [128, NTMAX], I32)
        pool_turns = ctx.enter_context(nc.semaphore("pool_turns"))
        env = {"pool_turns": pool_turns, "X": X, "aff": affs, "alpha": alpha, "share": share, "slots": slots, "toks": toks, "tile_e": tile_e}
        env["w1"] = sb("w1", [128, E, DC, F])
        consts = {n: t[n] for n in ("ident", "before", "pref", "starts", "tile_no", "row_no", "seq_no", "tok_no")}
        for layer in range(2):
            NT = (NT0, NT1)[layer]
            ys = nc.dram_tensor(f"tile_rows{layer}", (NT * 128, D), F32, kind="Internal").ap()
            mine = {n[3:]: a for n, a in t.items() if n.startswith(f"A{layer}_")}
            io = {"x": t["x"], "ctx": t["ctx"], "keep": t["keep"], "ys": t.get("ys"), "w1": t[f"E{layer}_w1"]}
            env["slots"] = slots[0]
            attention(nc, layer, {**consts, **io, **mine}, env)
            env["slots"] = slots
            mine = {n[3:]: a for n, a in t.items() if n.startswith(f"E{layer}_")}
            with ExitStack() as inner:
                if layer == 0:
                    second = inner.enter_context(nc.sbuf_tensor("w2", [128, E, FC, D], F32))
                    env["second"] = [(second[:, e], mine["w2"][:, e]) for e in range(E)]
                else:
                    second = inner.enter_context(nc.sbuf_tensor("b1_rows", [128, E, F], F32))
                    env["second"] = [(second[:], mine["b1"].partition_broadcast(128))]
                env["second_buf"] = second
                env["second_loaded"] = inner.enter_context(nc.semaphore(f"second_loaded{layer}"))
                routing(nc, layer, consts, env)
                expert_tiles(nc, layer, {**consts, "keep": t["keep"], "ys": ys, **mine}, env)
            t["ys"] = ys
        combine(nc, t, env)


def constants():
    import numpy as np

    p = np.arange(128)
    q = np.arange(LQ)
    rows = np.ones((128, 1), np.float32)
    return {
        "ident": np.eye(128, dtype=np.float32),
        "before": (q[:, None] < q[None, :]).astype(np.float32),
        "pref": rows * (E - np.arange(E, dtype=np.float32)),
        "starts": rows * (128 * np.arange(NTMAX, dtype=np.float32)),
        "tile_no": rows * np.arange(NTMAX, dtype=np.float32),
        "row_no": rows[0:LQ] * np.arange(128, dtype=np.float32),
        "seq_no": rows[0:LQ] * np.arange(NB, dtype=np.float32),
        "tok_no": q[:, None].astype(np.float32),
        "A0_mask": (p[:, None] // 16 == np.arange(8)[None, :]).astype(np.float32),
        "A1_mask": (p[:, None] // 32 == np.arange(4)[None, :]).astype(np.float32),
    }


def layouts(a):
    import numpy as np

    def chunks(w):
        return w.reshape(-1, 128, w.shape[-1]).transpose(1, 0, 2)

    def columns(v):
        return v.reshape(-1, 128).T

    kv = a["L0_xattn_Wkv"]
    bkv = a["L0_xattn_bkv"]
    d = {
        "x": a["x"],
        "ctx": a["ctx_1024"].reshape(NB, LK, DC, 128).transpose(0, 3, 2, 1),
        "A0_wq": chunks(a["L0_xattn_Wq"]), "A0_wk": chunks(kv[:, :D]), "A0_wv": chunks(kv[:, D:]),
        "A0_bq": columns(a["L0_xattn_bq"]), "A0_bk": columns(bkv[:D]), "A0_bv": bkv[D:],
        "A0_rows": a["L0_ffn_centroids"],
        "E0_lng": columns(a["L0_ffn_ln_g"]), "E0_lnb": columns(a["L0_ffn_ln_b"]),
        "E0_w1": a["L0_ffn_w1"].reshape(E, F, DC, 128).transpose(3, 0, 2, 1),
        "E0_b1": columns(a["L0_ffn_b1"]),
        "E0_w2": a["L0_ffn_w2"].reshape(E, D, FC, 128).transpose(3, 0, 2, 1),
        "E0_b2": a["L0_ffn_b2"],
        "A1_wq": chunks(a["L1_xattn_Wq"].T), "A1_wk": chunks(a["L1_xattn_Wk"].T),
        "A1_wv": chunks(a["L1_xattn_Wv"].T), "A1_wo": chunks(a["L1_xattn_Wo"].T),
        "A1_bq": columns(a["L1_xattn_bq"]), "A1_bk": columns(a["L1_xattn_bk"]), "A1_bv": a["L1_xattn_bv"],
        "A1_bq_row": a["L1_xattn_bq"], "A1_bo": a["L1_xattn_bo"],
        "A1_g0": a["L1_xattn_g0"], "A1_b0": a["L1_xattn_b0"], "A1_g1": a["L1_xattn_g1"], "A1_b1": a["L1_xattn_b1"],
        "A1_rows": a["L1_ffn_Wg"],
        "E1_w1": a["L1_ffn_W1"].reshape(E, F, DC, 128).transpose(3, 0, 2, 1),
        "E1_b1": a["L1_ffn_b1"],
        "E1_wo": chunks(a["L1_ffn_Wo"].T), "E1_b2": a["L1_ffn_bo"],
    }
    return {n: np.ascontiguousarray(v) for n, v in {**d, **constants()}.items()}


def kernel(**inputs):
    import numpy as np
    import concourse.bacc as bacc
    from concourse.bass_utils import run_bass_kernel_spmd

    nc = bacc.Bacc("TRN2", target_bir_lowering=False, num_devices=1)
    arrays = layouts({n: np.asarray(v) for n, v in inputs.items()})
    arrays = {f"in_{n}": v for n, v in arrays.items()}
    t = {n[3:]: nc.dram_tensor(n, v.shape, mybir.dt.from_np(v.dtype), kind="ExternalInput").ap()
         for n, v in arrays.items()}
    t["out"] = nc.dram_tensor("out", (NB, LQ, D), F32, kind="ExternalOutput").ap()
    program(nc, t)
    return run_bass_kernel_spmd(nc, [arrays], core_ids=[0]).results[0]["out"]
```

```python
from contextlib import ExitStack

import concourse.bass as bass
from concourse import mybir

ALU = mybir.AluOpType
ACT = mybir.ActivationFunctionType
F32 = mybir.dt.float32
BF16 = mybir.dt.bfloat16
F32R = mybir.dt.float32r
I32 = mybir.dt.int32
AX_X = mybir.AxisListType.X

NB, LQ, LK, D = 32, 100, 361, 256
DC = D // 128
KTILES = [(0, 121), (121, 120), (241, 120)]
E = 8
F = 1024
FC = F // 128
GH = F // 2
TOK = NB * LQ
LN_EPS = 1e-5


def slot_tiles(pairs):
    return (pairs + E * 127) // 128


NT0 = slot_tiles(TOK)
NT1 = slot_tiles(2 * TOK)
NTMAX = 64


class Batch:

    def __init__(self, r, p, low):
        self.r, self.p, self.low = r, p, low

    def count(self, n, c=0):
        return self.r * (2 * n) + (self.p * n + c)

    @property
    def at(self):
        return self.r * 2 + self.p

    def plus(self, k):
        q = self.p + k
        return Batch(self.r + q // 2, q % 2, self.low + k)


def fixed(b):
    return Batch(b // 2, b % 2, b)


LOOP_FROM, LOOP_TO = 4, NB - 4


def run_steps(engine, step):

    def peeled(t):
        step(fixed(t + 2).plus(-2), 0 <= t + 1 < NB, t + 2 < NB, 0 <= t < NB, 0 <= t - 1 < NB)

    for t in range(-1, LOOP_FROM):
        peeled(t)
    with engine.Fori(LOOP_FROM // 2, LOOP_TO // 2) as i:
        for p in range(2):
            step(Batch(i, p, LOOP_FROM + p), True, True, True, True)
    for t in range(LOOP_TO, NB + 1):
        peeled(t)


def stage_semaphore(nc, sems, name):
    sems.append(nc.alloc_semaphore(name=name))
    return sems[-1]


def end_stage(nc, sems):
    nc.clear_and_free_semaphores(sems)
    nc.all_engine_barrier()


class Links:

    def __init__(self, engine, sem):
        self.engine, self.sem, self.base, self.n = engine, sem, 0, 0

    def __call__(self, instruction):
        instruction.then_inc(self.sem, 1)
        self.n += 1
        self.engine.wait_ge(self.sem, self.base + self.n)


def attention(nc, layer, t, env):
    H = 16 if layer == 0 else 8
    HD = D // H
    NH2 = H // 2
    VW = 32 if layer == 0 else 64
    HG = 128 // VW
    NG = H // HG
    NP = H // 2
    SLOTS = [(kt, s) for s in range(H // 8) for kt in range(3)]
    NS = len(SLOTS)
    SCALE = 0.25 if layer == 0 else 1.0 / 16.0
    X = env["X"]
    tag = f"a{layer}_"

    sems = []
    with ExitStack() as ctx:
        def sb(name, shape, dt=F32):
            return ctx.enter_context(nc.sbuf_tensor(tag + name, shape, dt))

        def sem(name):
            return stage_semaphore(nc, sems, tag + name)

        wq = sb("wq", [128, DC, D])
        wk = sb("wk", [128, DC, D])
        wv = sb("wv", [128, DC, D])
        bq = sb("bq", [128, DC])
        bk = sb("bk", [128, DC])
        bvb = sb("bvb", [LQ, D])
        ident = sb("ident", [128, 128])
        neg_ident = sb("neg_ident", [LQ, LQ], BF16)
        ones_bf = sb("ones_bf", [LQ, 128], BF16)
        mask = sb("mask", [128, NH2])
        half_neg = sb("half_neg", [LQ, 1])
        ct = [sb(f"ct{p}", [128, DC, LK]) for p in range(2)]
        xh = sb("xh", [LQ, D])
        xT = sb("xT", [128, DC, LQ])
        qf = sb("qf", [128, DC, LQ])
        q_hi = sb("q_hi", [128, DC, LQ], F32R)
        q_lo = sb("q_lo", [128, DC, LQ])
        QM = [sb(f"QM{p}", [128, H, LQ], F32R) for p in range(2)]
        QL = sb("QL", [128, H, LQ], F32R)
        QMb = sb("QMb", [128, H, LQ], BF16)
        KF = sb("KF", [128, DC, LK])
        KT = [sb(f"KT{p}", [128, DC, LK], F32R) for p in range(2)]
        KL = [sb(f"KL{p}", [128, DC, LK], F32R) for p in range(2)]
        KTb = sb("KTb", [128, DC, LK], BF16)
        V = [sb(f"V{p}", [128, 3, H, VW]) for p in range(2)]
        mx = sb("mx", [LQ, H])
        DM = sb("DM", [LQ, H, LQ], BF16)
        Pr = sb("Pr", [128, 3, H * LQ])
        avs = sb("avs", [128, NG, LQ])
        rs = sb("rs", [LQ, H])
        o = sb("o", [LQ, D])
        st = sb("st", [LQ, 6])
        NL = 3 if layer == 0 else 4
        mv = [sb(f"mv{k}", [LQ, 2]) for k in range(NL)]
        ve = [sb(f"ve{k}", [LQ, 1]) for k in range(NL)]
        rstd = [sb(f"rstd{k}", [LQ, 1]) for k in range(NL)]
        xp = sb("xp", [LQ, D])
        keep = sb("keep", [LQ, D])
        if layer == 0:
            rows = sb("rows", [LQ, E, D])
            junk = sb("junk", [LQ, 5, D])
            aff = sb("aff", [LQ, E])
        else:
            rows = sb("rows", [128, DC, E])
            bqb = sb("bqb", [LQ, D])
            wo = sb("wo", [128, DC, D])
            g0b, b0b, g1b, b1b, bob = (sb(n, [LQ, D]) for n in ("g0b", "b0b", "g1b", "b1b", "bob"))
            qtok = [sb(f"qtok{p}", [LQ, D]) for p in range(2)]
            o1 = sb("o1", [LQ, D])
            o2 = sb("o2", [LQ, D])
            o3 = sb("o3", [LQ, D])
            oT = sb("oT", [128, 2 * DC, LQ])
            yg = [sb(f"yg{p}", [LQ, D]) for p in range(2)]
            gidx = [sb(f"gidx{p}", [LQ, 1], I32) for p in range(2)]

        ST = ctx.enter_context(nc.psum_tensor(tag + "ST", [128, 2, 2, 512], F32))
        SM = ctx.enter_context(nc.psum_tensor(tag + "SM", [128, 2, 512], F32))
        M0 = ctx.enter_context(nc.psum_tensor(tag + "M0", [128, 512], F32))
        M1 = ctx.enter_context(nc.psum_tensor(tag + "M1", [128, 512], F32))

        wk_loaded = sem("wk_loaded")
        loaded = sem("loaded")
        rest_loaded = sem("rest_loaded")
        x_loaded = sem("x_loaded")
        x_rest_loaded = sem("x_rest_loaded")
        ct_loaded = [sem(f"ct_loaded{p}") for p in range(2)]
        pads_set = sem("pads_set")
        xh_ready = sem("xh_ready")
        xT_ps = sem("xT_ps")
        xT_sb = sem("xT_sb")
        q_ps = sem("q_ps")
        k_ps = sem("k_ps")
        v_ps = sem("v_ps")
        qf_ready = sem("qf_ready")
        q_hi_ready = sem("q_hi_ready")
        q_lo_ready = sem("q_lo_ready")
        ql_ready = sem("ql_ready")
        kt_ready = sem("kt_ready")
        kl_ready = sem("kl_ready")
        qm_ready = sem("qm_ready")
        qmb_ready = sem("qmb_ready")
        k_evac = sem("k_evac")
        ktb_ready = sem("ktb_ready")
        v_evac = sem("v_evac")
        qtok_ready = sem("qtok_ready")
        qtok_used = sem("qtok_used")
        sm_ps = sem("sm_ps")
        max_done = sem("max_done")
        dm_ready = sem("dm_ready")
        st_ps = sem("st_ps")
        exp_done = sem("exp_done")
        av_ps = sem("av_ps")
        avs_copied = sem("avs_copied")
        avt_ps = sem("avt_ps")
        norm_read = sem("norm_read")
        var_ready = [sem(f"var_ready{k}") for k in range(NL)]
        rstd_ready = [sem(f"rstd_ready{k}") for k in range(NL)]
        keep_ready = sem("keep_ready")
        keep_stored = sem("keep_stored")
        w1_loaded = sem("w1_loaded")
        dve_own = [sem(f"dve_own{k}") for k in range(3)]
        dve_turns = sem("dve_turns")
        pool_turns = env["pool_turns"]
        o1_ready = sem("o1_ready")
        o3_ready = sem("o3_ready")
        x3_ready = sem("x3_ready")
        oT_ps = sem("oT_ps")
        oT_sb = sem("oT_sb")
        wo_ps = sem("wo_ps")
        wo_used = sem("wo_used")
        yg_loaded = [sem(f"yg_loaded{p}") for p in range(2)]
        x2_done = sem("x2_done")
        gidx_ready = sem("gidx_ready")

        first = [(bq, t["bq"]), (bk, t["bk"]), (ident, t["ident"]), (mask, t["mask"]), (wq, t["wq"]), (wv, t["wv"])]
        rest = [(bvb, t["bv"].partition_broadcast(LQ)), (rows, t["rows"] if layer else t["rows"].partition_broadcast(LQ))]
        if layer == 1:
            rest += [(wo, t["wo"]), (bqb, t["bq_row"].partition_broadcast(LQ))]
            rest += [(w, t[n].partition_broadcast(LQ))
                     for w, n in ((g0b, "g0"), (b0b, "b0"), (g1b, "g1"), (b1b, "b1"), (bob, "bo"))]
        FIRST_LOADED = 16 * len(first)
        REST_LOADED = 16 * len(rest)

        block = ctx.enter_context(nc.Block())

        @block.sync
        def _(sp):
            def load(b):
                if b.low >= 2:
                    sp.wait_ge(v_ps, b.count(2, -2))
                sp.dma_start(ct[b.p][:], t["ctx"][bass.ds(b.at, 1)].rearrange("o p c k -> p (o c) k")
                             ).then_inc(ct_loaded[b.p], 16)

            def store(b):
                sp.wait_ge(keep_ready, b.count(1, 1))
                sp.dma_start(t["keep"][bass.ds(b.at * LQ, LQ), :], keep[:]).then_inc(keep_stored, 16)

            if layer == 0:
                sp.dma_start(X[:, 0:4], t["x"][0:4].rearrange("b q d -> q b d")).then_inc(x_loaded, 16)
            sp.dma_start(wk[:], t["wk"]).then_inc(wk_loaded, 16)
            load(fixed(0))
            for dst, src in first:
                sp.dma_start(dst[:], src).then_inc(loaded, 16)
            load(fixed(1))
            for dst, src in rest:
                sp.dma_start(dst[:], src).then_inc(rest_loaded, 16)
            if layer == 0:
                sp.dma_start(X[:, 4:NB], t["x"][4:NB].rearrange("b q d -> q b d")).then_inc(x_rest_loaded, 16)
            for b in range(2, 4):
                load(fixed(b))
            with sp.Fori(0, E) as i:
                for p in range(2):
                    load(Batch(i + 2, p, 4 + p))
                    store(Batch(i, p, p))
                sp.dma_start(env["w1"][:, bass.ds(i, 1)].rearrange("p o c f -> p (o c f)"),
                             t["w1"][:, bass.ds(i, 1)].rearrange("p o c f -> p (o c f)")).then_inc(w1_loaded, 16)
            with sp.Fori(E, (NB - 4) // 2) as i:
                for p in range(2):
                    load(Batch(i + 2, p, 4 + p))
                    store(Batch(i, p, p))
            for b in range(NB - 4, NB):
                store(fixed(b))
            sp.wait_ge(keep_stored, 16 * NB)
            sp.wait_ge(w1_loaded, 16 * E)

        @block.tensor
        def _(pe):
            def project_k(b, h):
                for c in range(DC):
                    last = nc.tensor.matmul(M1[:, 0:LK], wk[:, c, h * 128:(h + 1) * 128], ct[b.p][:, c, :],
                                            start=(c == 0), stop=(c == DC - 1))
                last.then_inc(k_ps, 1)

            def project_v(b, kt, M, c0):
                k0, n = KTILES[kt]
                for c in range(DC):
                    last = nc.tensor.matmul(M[0:n, c0:c0 + D], ct[b.p][:, c, k0:k0 + n], wv[:, c, :],
                                            start=(c == 0), stop=(c == DC - 1))
                return last

            def first_k(b):
                pe.wait_ge(ct_loaded[b.p], b.r * 16 + 16)
                project_k(b, 0)

            def front(b):
                pe.wait_ge(xh_ready, b.count(1, 1))
                if b.low == 1:
                    pe.wait_ge(v_evac, 2)
                    if layer == 1:
                        pe.wait_ge(qtok_ready, 1)
                for c in range(DC):
                    last = nc.tensor.transpose(M0[:, c * LQ:(c + 1) * LQ], xh[:, c * 128:(c + 1) * 128],
                                               ident[0:LQ, 0:LQ])
                last.then_inc(xT_ps, 1)
                pe.wait_ge(k_evac, b.count(2, 1))
                project_k(b, 1)
                pe.wait_ge(xT_sb, b.count(1, 1))
                for h in range(DC):
                    for c in range(DC):
                        last = nc.tensor.matmul(M0[:, h * LQ:(h + 1) * LQ], wq[:, c, h * 128:(h + 1) * 128],
                                                xT[:, c, :], start=(c == 0), stop=(c == DC - 1))
                last.then_inc(q_ps, 1)
                pe.wait_ge(k_evac, b.count(2, 2))
                project_v(b, 1, M1, 0)
                project_v(b, 2, M1, D).then_inc(v_ps, 1)

            def front_end(b):
                pe.wait_ge(qf_ready, b.count(1, 1))
                last = project_v(b, 0, M0, 0)
                if layer == 1:
                    for c in range(DC):
                        last = nc.tensor.matmul(M0[0:LQ, D:2 * D], xT[:, c, :], wq[:, c, :],
                                                start=(c == 0), stop=(c == DC - 1))
                last.then_inc(v_ps, 1)

            def score_rows(b, j):
                if j == 0:
                    pe.wait_ge(ktb_ready, b.count(2, 2))
                if j % (NP // 2) == 0:
                    pe.wait_ge(qmb_ready, b.count(2, 1 + j // (NP // 2)))
                pe.wait_ge(max_done, b.count(NP, j))
                for h in (2 * j, 2 * j + 1):
                    last = nc.tensor.matmul(SM[0:LQ, h % 2, 0:LK], QMb[:, h, :], KTb[:, h // NH2, :],
                                            start=True, stop=True)
                last.then_inc(sm_ps, 1)

            def scores(b, s):
                kt, eight = SLOTS[s]
                k0, n = KTILES[kt]
                buf = (b.p * NS + s) % 2
                if s == 0:
                    pe.wait_ge(dm_ready, b.count(1, 1))
                    pe.wait_ge(ql_ready, b.count(1, 1))
                    pe.wait_ge(kl_ready, b.count(1, 1))
                    if b.low >= 1:
                        pe.wait_ge(norm_read, b.count(1))
                if b.low >= 1 or s >= 2:
                    pe.wait_ge(exp_done, b.count(NS, s - 1))
                for j in range(2):
                    h = 8 * eight + 4 * j
                    out = ST[0:n, buf, j, 0:4 * LQ]
                    high, low = (K[b.p][:, h // NH2, k0:k0 + n] for K in (KT, KL))
                    nc.tensor.matmul(out, high, QM[b.p][:, h:h + 4, :], start=True, stop=False)
                    nc.tensor.matmul(out, high, QL[:, h:h + 4, :], start=False, stop=False)
                    nc.tensor.matmul(out, low, QM[b.p][:, h:h + 4, :], start=False, stop=False)
                    last = nc.tensor.matmul(ST[0:n, buf, j, 0:4 * LQ], ones_bf[:, 0:n],
                                            DM[:, h:h + 4, :], start=False, stop=True)
                last.then_inc(st_ps, 1)

            def values(b, g, last_exps=False):
                for kt in range(3):
                    n = KTILES[kt][1]
                    if last_exps and kt == 2:
                        pe.wait_ge(exp_done, b.count(NS, NS))
                    for j in range(HG):
                        h = g * HG + j
                        last = nc.tensor.matmul(M0[VW * j:VW * (j + 1), g * LQ:(g + 1) * LQ],
                                                V[b.p][0:n, kt, h, :], Pr[0:n, kt, h * LQ:(h + 1) * LQ],
                                                start=(kt == 0), stop=(kt == 2))
                return last

            def out_transposes(b, out, routed):
                if out:
                    pe.wait_ge(o1_ready, b.count(1, 1))
                    for c in range(DC):
                        last = nc.tensor.transpose(M1[:, c * LQ:(c + 1) * LQ], o1[:, c * 128:(c + 1) * 128],
                                                   ident[0:LQ, 0:LQ])
                if routed:
                    pe.wait_ge(keep_ready, b.count(1, -1))
                    for c in range(DC):
                        last = nc.tensor.transpose(M1[:, (DC + c) * LQ:(DC + c + 1) * LQ],
                                                   keep[:, c * 128:(c + 1) * 128], ident[0:LQ, 0:LQ])
                last.then_inc(oT_ps, 1)

            def out_product(b, out, routed):
                if b.low == 0:
                    pe.wait_ge(rest_loaded, REST_LOADED)
                pe.wait_ge(oT_sb, b.count(1, 1))
                for c in range(DC):
                    if out:
                        last = nc.tensor.matmul(M1[0:LQ, 0:D], oT[:, c, :], wo[:, c, :],
                                                start=(c == 0), stop=(c == DC - 1))
                for c in range(DC):
                    if routed:
                        last = nc.tensor.matmul(M1[0:LQ, 2 * DC * LQ:2 * DC * LQ + E], oT[:, DC + c, :], rows[:, c, :],
                                                start=(c == 0), stop=(c == DC - 1))
                last.then_inc(wo_ps, 1)

            def free_m0(nxt, fr):
                if fr:
                    pe.wait_ge(v_evac, nxt.count(2, 2))
                    if layer == 1:
                        pe.wait_ge(qtok_ready, nxt.count(1, 1))

            def start_k(nxt, nxt2, prev, tail):
                pe.wait_ge(v_evac, nxt.count(2, 1))
                if layer == 1 and tail:
                    pe.wait_ge(wo_used, prev.count(1, 1))
                first_k(nxt2)

            EARLY = 1 if layer == 0 else 0
            EARLY_EXPS = 2 if layer == 0 else 0

            def step(b, fr, ahead, back, tail):
                nxt, nxt2, prev = b.plus(1), b.plus(2), b.plus(-1)
                if fr:
                    front(nxt)
                if back:
                    scores(b, 0)
                if fr:
                    front_end(nxt)
                pair = 0
                for s in range(NS):
                    if back:
                        if s == 4:
                            pe.wait_ge(exp_done, b.count(NS, 3))
                            free_m0(nxt, fr)
                            values(b, 0)
                        if s > 0:
                            scores(b, s)
                    if fr:
                        score_rows(nxt, pair)
                        pair += 1
                    if layer == 1 and tail and s == 2:
                        if fr:
                            pe.wait_ge(v_evac, nxt.count(2, 1))
                        out_transposes(prev, True, prev.low >= 2)
                for g in range(EARLY, NG):
                    if back:
                        late = g == max(EARLY, EARLY_EXPS)
                        if late:
                            pe.wait_ge(exp_done, b.count(NS, NS - 1))
                        if g == 0:
                            free_m0(nxt, fr)
                        last = values(b, g, late)
                    if layer == 1 and tail and g == 1:
                        out_product(prev, True, prev.low >= 2)
                    if fr and layer == 0 and g == 2:
                        score_rows(nxt, 6)
                if back:
                    last.then_inc(av_ps, 1)
                if ahead:
                    start_k(nxt, nxt2, prev, tail)
                if fr:
                    score_rows(nxt, NP - 1)
                if back:
                    pe.wait_ge(avs_copied, b.count(1, 1))
                    for g in range(NG):
                        last = nc.tensor.transpose(ST[0:LQ, 0, 0, g * 128:(g + 1) * 128], avs[:, g, :], ident[:])
                    last.then_inc(avt_ps, 1)

            pe.wait_ge(wk_loaded, 16)
            first_k(fixed(0))
            pe.wait_ge(loaded, FIRST_LOADED)
            pe.wait_ge(pads_set, 4)
            run_steps(pe, step)
            if layer == 1:
                for b in (NB, NB + 1):
                    pe.wait_ge(wo_used, b)
                    out_transposes(fixed(b), False, True)
                    out_product(fixed(b), False, True)

        @block.scalar
        def _(act):
            def copy_k(b, h):
                act.wait_ge(kl_ready, b.count(1))
                act.wait_ge(ktb_ready, b.count(2))
                act.wait_ge(k_ps, b.count(2, h + 1))
                nc.scalar.activation(KF[:, h, :], M1[:, 0:LK], ACT.Identity, bias=bk[:, h:h + 1]
                                     ).then_inc(k_evac, 1)

            def split_k(b):
                act.wait_ge(k_evac, b.count(2, 2))
                if b.low >= 2:
                    act.wait_ge(st_ps, b.count(NS, -NS))
                nc.scalar.activation(KT[b.p][:], KF[:], ACT.Copy).then_inc(kt_ready, 1)
                act.wait_ge(sm_ps, b.count(NP))
                nc.scalar.activation(KTb[:], KF[:], ACT.Copy).then_inc(ktb_ready, 2)

            def copy_v(b, kt, M, c0):
                n = KTILES[kt][1]
                return nc.scalar.activation(V[b.p][0:n, kt, :, 0:HD],
                                            M[0:n, c0:c0 + D].rearrange("p (h d) -> p h d", h=H), ACT.Copy)

            def front(b):
                act.wait_ge(v_ps, b.count(2))
                act.wait_ge(xT_ps, b.count(1, 1))
                nc.scalar.activation(xT[:], M0[:, 0:DC * LQ].rearrange("p (c q) -> p c q", c=DC), ACT.Copy
                                     ).then_inc(xT_sb, 1)
                copy_k(b, 1)
                act.wait_ge(q_ps, b.count(1, 1))
                act.wait_ge(qm_ready, b.count(2))
                act.wait_ge(q_lo_ready, b.count(1))
                for h in range(DC):
                    last = nc.scalar.activation(qf[:, h, :], M0[:, h * LQ:(h + 1) * LQ], ACT.Identity,
                                                bias=bq[:, h:h + 1])
                last.then_inc(qf_ready, 1)
                split_k(b)
                for h in range(DC):
                    half = slice(h * NH2, (h + 1) * NH2)
                    act.wait_ge(qm_ready, b.count(2, h + 1))
                    nc.scalar.activation(QMb[:, half, :], QM[b.p][:, half, :], ACT.Copy).then_inc(qmb_ready, 1)
                if b.low >= 2:
                    act.wait_ge(av_ps, b.count(1, -1))
                act.wait_ge(v_ps, b.count(2, 1))
                copy_v(b, 1, M1, 0)
                copy_v(b, 2, M1, D).then_inc(v_evac, 1)
                act.wait_ge(v_ps, b.count(2, 2))
                copy_v(b, 0, M0, 0).then_inc(v_evac, 1)
                if layer == 1:
                    if b.low >= 2:
                        act.wait_ge(qtok_used, b.count(1, -1))
                    nc.scalar.activation(qtok[b.p][:], M0[0:LQ, D:2 * D], ACT.Copy).then_inc(qtok_ready, 1)

            def copy_out(b, c0, c1):
                act.wait_ge(oT_ps, b.count(1, 1))
                act.wait_ge(wo_ps, b.count(1))
                nc.scalar.activation(oT[:, c0:c1, :], M1[:, c0 * LQ:c1 * LQ].rearrange("p (c q) -> p c q", q=LQ),
                                     ACT.Copy).then_inc(oT_sb, 1)

            def step(b, fr, ahead, back, tail):
                if fr:
                    front(b.plus(1))
                if back:
                    act.wait_ge(av_ps, b.count(1))
                for s, (kt, eight) in enumerate(SLOTS):
                    if back:
                        n = KTILES[kt][1]
                        act.wait_ge(st_ps, b.count(NS, s + 1))
                        dst = Pr[0:n, kt, eight * 8 * LQ:(eight + 1) * 8 * LQ]
                        nc.scalar.activation(dst.rearrange("p (j q) -> p j q", j=2),
                                             ST[0:n, (b.p * NS + s) % 2, :, 0:4 * LQ], ACT.Exp, scale=SCALE
                                             ).then_inc(exp_done, 1)
                    if layer == 1 and tail and s == 2:
                        prev = b.plus(-1)
                        copy_out(prev, 0, 2 * DC if prev.low >= 2 else DC)
                if back:
                    act.wait_ge(av_ps, b.count(1, 1))
                    act.wait_ge(avt_ps, b.count(1))
                    nc.scalar.activation(avs[:], M0[:, 0:NG * LQ].rearrange("p (g q) -> p g q", g=NG), ACT.Copy
                                         ).then_inc(avs_copied, 1)
                if ahead:
                    copy_k(b.plus(2), 0)

            act.wait_ge(loaded, FIRST_LOADED)
            act.wait_ge(pads_set, 4)
            copy_k(fixed(0), 0)
            run_steps(act, step)
            if layer == 1:
                for b in (NB, NB + 1):
                    copy_out(fixed(b), DC, 2 * DC)

        @block.gpsimd
        def _(pool):
            def wait_apart():
                pool.sem_inc(pool_turns, 1)

            def power(k, b):
                pool.wait_ge(var_ready[k], b.count(1, 1))
                nc.gpsimd.tensor_tensor(rstd[k][:], ve[k][:], half_neg[:], ALU.pow).then_inc(rstd_ready[k], 1)

            def gather(b):
                if b.low >= 2:
                    pool.wait_ge(x2_done, b.count(1, -1))
                wait_apart()
                nc.gpsimd.tensor_copy(gidx[b.p][:], env["slots"][:, bass.ds(b.at, 1)]).then_inc(gidx_ready, 1)
                pool.wait_ge(gidx_ready, b.count(1, 1))
                wait_apart()
                nc.gpsimd.indirect_dma_start(yg[b.p][:], None, t["ys"], bass.IndirectOffsetOnAxis(gidx[b.p][:], 0)
                                             ).then_inc(yg_loaded[b.p], 16)

            def low_parts(b):
                pool.wait_ge(kt_ready, b.count(1, 1))
                if b.low >= 2:
                    pool.wait_ge(st_ps, b.count(NS, -NS))
                nc.gpsimd.tensor_tensor(KL[b.p][:], KF[:], KT[b.p][:], ALU.subtract).then_inc(kl_ready, 1)
                pool.wait_ge(q_hi_ready, b.count(1, 1))
                pool.wait_ge(ql_ready, b.count(1))
                nc.gpsimd.tensor_tensor(q_lo[:], qf[:], q_hi[:], ALU.subtract).then_inc(q_lo_ready, 1)

            def masked_low(b):
                pool.wait_ge(q_lo_ready, b.count(1, 1))
                pool.wait_ge(st_ps, b.count(NS))
                nc.gpsimd.tensor_tensor(
                    QL[:].rearrange("p (c h) q -> p c h q", c=DC),
                    q_lo[:].unsqueeze(2).to_broadcast([128, DC, NH2, LQ]),
                    mask[:].unsqueeze(1).unsqueeze(3).to_broadcast([128, DC, NH2, LQ]), ALU.mult).then_inc(ql_ready, 1)

            def diagonals(b):
                pool.wait_ge(max_done, b.count(NP, NP))
                pool.wait_ge(st_ps, b.count(NS))
                nc.gpsimd.tensor_tensor(DM[:], neg_ident[:].unsqueeze(1).to_broadcast([LQ, H, LQ]),
                                        mx[:].unsqueeze(2).to_broadcast([LQ, H, LQ]), ALU.mult
                                        ).then_inc(dm_ready, 1)

            def residual1(b):
                row = X[:, bass.ds(b.at, 1), :].rearrange("q o d -> q (o d)")
                pool.wait_ge(o3_ready, b.count(1, 1))
                nc.gpsimd.tensor_tensor(row, row, o3[:], ALU.add).then_inc(x3_ready, 1)

            def step(b, fr, ahead, back, tail):
                nxt, nxt2, prev, prev2 = b.plus(1), b.plus(2), b.plus(-1), b.plus(-2)
                ends = layer == 1 and tail and prev2.low >= 0
                if fr:
                    low_parts(nxt)
                if tail:
                    power(1, prev)
                if ends:
                    residual1(prev2)
                if tail and layer == 0:
                    power(2, prev)
                if ahead:
                    power(0, nxt2)
                if ends:
                    power(3, prev2)
                if fr:
                    masked_low(nxt)
                    diagonals(nxt)
                if tail and layer == 1:
                    power(2, prev)
                if ahead and layer == 1 and nxt2.low + 1 < NB:
                    gather(nxt2.plus(1))

            if layer == 1:
                gather(fixed(0))
                gather(fixed(1))
            nc.gpsimd.memset(half_neg[:], -0.5)
            nc.gpsimd.memset(ones_bf[:], 1.0).then_inc(pads_set, 1)
            for p in range(2):
                nc.gpsimd.memset(V[p][:], 0.0).then_inc(pads_set, 1)
            pool.wait_ge(loaded, FIRST_LOADED)
            pool.wait_ge(pads_set, 3)
            for p in range(2):
                nc.gpsimd.memset(V[p][:, :, :, HD:HD + 1], 1.0)
            nc.gpsimd.tensor_scalar(neg_ident[:], ident[0:LQ, 0:LQ], -1.0, 0.0, ALU.mult, ALU.add
                                    ).then_inc(pads_set, 1)
            pool.wait_ge(pads_set, 4)
            power(0, fixed(0))
            run_steps(pool, step)
            if layer == 1:
                residual1(fixed(NB - 1))
                power(3, fixed(NB - 1))

        @block.vector
        def _(dve):
            V_ = nc.vector
            link = Links(dve, dve_own[0])

            def wait_apart():
                dve.sem_inc(dve_turns, 1)

            def norm_stats(k, b, src):
                wait_apart()
                link(V_.bn_stats(st[:], src))
                wait_apart()
                link(V_.bn_aggr(mv[k][:], st[:]))
                V_.tensor_scalar(ve[k][:], mv[k][:, 1:2], LN_EPS, None, ALU.add).then_inc(var_ready[k], 1)

            def rstd_of(k, b):
                dve.wait_ge(rstd_ready[k], b.count(1, 1))

            def normed(out, k, src):
                return V_.tensor_scalar(out, src, mv[k][:, 0:1], rstd[k][:], ALU.subtract, ALU.mult)

            def xrow(b):
                return X[:, bass.ds(b.at, 1), :].rearrange("q o d -> q (o d)")

            def input_stats(b):
                if layer == 1:
                    dve.wait_ge(yg_loaded[b.p], b.r * 16 + 16)
                    V_.scalar_tensor_tensor(xrow(b), yg[b.p][:], env["alpha"][:, bass.ds(b.at, 1)], xrow(b),
                                            ALU.mult, ALU.add).then_inc(x2_done, 1)
                    dve.wait_ge(x2_done, b.count(1, 1))
                norm_stats(0, b, xrow(b))

            def input_rows(b):
                rstd_of(0, b)
                dve.wait_ge(xT_ps, b.count(1))
                normed(xh[:], 0, xrow(b)).then_inc(xh_ready, 1)

            def masked_queries(b):
                dve.wait_ge(qf_ready, b.count(1, 1))
                if b.low >= 2:
                    dve.wait_ge(st_ps, b.count(NS, -NS))
                    dve.wait_ge(qmb_ready, b.count(2, -2))
                for h in range(DC):
                    V_.tensor_tensor(
                        QM[b.p][:, h * NH2:(h + 1) * NH2, :], qf[:, h, :].unsqueeze(1).to_broadcast([128, NH2, LQ]),
                        mask[:].unsqueeze(2).to_broadcast([128, NH2, LQ]), ALU.mult).then_inc(qm_ready, 1)
                dve.wait_ge(q_lo_ready, b.count(1))
                V_.tensor_copy(q_hi[:], qf[:]).then_inc(q_hi_ready, 1)

            def maxima(b, j):
                if j == 0:
                    dve.wait_ge(dm_ready, b.count(1))
                dve.wait_ge(sm_ps, b.count(NP, j + 1))
                V_.tensor_reduce(mx[:, 2 * j:2 * j + 2], SM[0:LQ, :, 0:LK], AX_X, ALU.max
                                 ).then_inc(max_done, 1)

            def normalise(b):
                dve.wait_ge(avt_ps, b.count(1, 1))
                mm = ST[0:LQ, 0, 0, :].rearrange("q (h w) -> q h w", h=H)
                link(V_.reciprocal(rs[:], mm[:, :, HD]))
                V_.tensor_tensor(o[:].rearrange("q (h d) -> q h d", h=H), mm[:, :, 0:HD],
                                 rs[:].unsqueeze(2).to_broadcast([LQ, H, HD]), ALU.mult).then_inc(norm_read, 1)

            def residual(b):
                dve.wait_ge(norm_read, b.count(1, 1))
                if b.low == 0:
                    dve.wait_ge(rest_loaded, REST_LOADED)
                    if layer == 0:
                        dve.wait_ge(x_rest_loaded, 16)
                    else:
                        link(V_.tensor_tensor(bqb[:], bqb[:], bvb[:], ALU.add))
                if layer == 0:
                    link(V_.tensor_tensor(o[:], o[:], bvb[:], ALU.add))
                    link(V_.tensor_tensor(xrow(b), xrow(b), o[:], ALU.add))
                else:
                    dve.wait_ge(qtok_ready, b.count(1, 1))
                    V_.tensor_tensor(o[:], o[:], qtok[b.p][:], ALU.add).then_inc(qtok_used, 1)
                    dve.wait_ge(qtok_used, b.count(1, 1))
                    link(V_.tensor_tensor(o[:], o[:], bqb[:], ALU.add))

            def residual_stats(b):
                norm_stats(1, b, xrow(b) if layer == 0 else o[:])

            def router(b, src, e0, e1):
                for e in range(e0, e1):
                    ins = V_.tensor_tensor_reduce(out=junk[:, e % 5, :], in0=src, in1=rows[:, e, :], scale=1.0,
                                                  scalar=0.0, op0=ALU.mult, op1=ALU.add,
                                                  accum_out=aff[:, e:e + 1])
                link(ins)
                if e1 == E:
                    link(V_.tensor_copy(env["aff"][:, bass.ds(b.at, 1), :].rearrange("q o e -> q (o e)"), aff[:]))

            def kept(b, k, src):
                rstd_of(k, b)
                dve.wait_ge(keep_stored, b.count(16))
                normed(keep[:], k, src).then_inc(keep_ready, 1)

            def tail0(b, j):
                if j == 0:
                    residual_stats(b)
                elif j == 1:
                    rstd_of(1, b)
                    link(normed(xp[:], 1, xrow(b)))
                    norm_stats(2, b, xp[:])
                elif j == 2:
                    kept(b, 2, xp[:])
                    link(V_.tensor_tensor(xrow(b), xrow(b), xp[:], ALU.add))
                elif j == 4:
                    router(b, xp[:], 0, 2)
                elif j == 5:
                    router(b, xp[:], 2, 3)
                elif j == 6:
                    router(b, xp[:], 3, 5)

            def scaled(out, k, src, gain):
                return V_.scalar_tensor_tensor(out, src, mv[k][:, 0:1], gain, ALU.subtract, ALU.mult)

            def shifted(out, k, shift):
                return V_.scalar_tensor_tensor(out, out, rstd[k][:], shift, ALU.mult, ALU.add)

            def tail1a(b):
                dve.wait_ge(oT_ps, b.count(1))
                dve.wait_ge(wo_used, b.count(1))
                link(scaled(o1[:], 1, o[:], g0b[:]))

            def tail1c(b):
                rstd_of(1, b)
                shifted(o1[:], 1, b0b[:]).then_inc(o1_ready, 1)
                dve.wait_ge(o1_ready, b.count(1, 1))

            def take_product(b, out, routed):
                dve.wait_ge(wo_ps, b.count(1, 1))
                if out:
                    last = V_.tensor_tensor(o2[:], M1[0:LQ, 0:D], bob[:], ALU.add)
                if routed:
                    last = V_.tensor_copy(
                        env["aff"][:, bass.ds(b.plus(-2).at, 1), :].rearrange("q o e -> q (o e)"),
                        M1[0:LQ, 2 * DC * LQ:2 * DC * LQ + E])
                last.then_inc(wo_used, 1)

            def tail1b(b):
                dve.wait_ge(wo_used, b.count(1, 1))
                link(V_.scalar_tensor_tensor(o2[:], o2[:], 0.0, o1[:], ALU.max, ALU.add))
                norm_stats(2, b, o2[:])
                dve.wait_ge(x3_ready, b.count(1))
                link(scaled(o3[:], 2, o2[:], g1b[:]))

            def end1(b, part):
                if part == 0:
                    rstd_of(2, b)
                    shifted(o3[:], 2, b1b[:]).then_inc(o3_ready, 1)
                elif part == 1:
                    dve.wait_ge(x3_ready, b.count(1, 1))
                    norm_stats(3, b, xrow(b))
                else:
                    if b.low >= 1:
                        dve.wait_ge(oT_ps, b.count(1, 2))
                    kept(b, 3, xrow(b))

            def step0(b, fr, ahead, back, tail):
                nxt, nxt2, prev = b.plus(1), b.plus(2), b.plus(-1)
                if fr:
                    masked_queries(nxt)
                if tail:
                    residual(prev)
                for j in range(NP):
                    if fr:
                        maxima(nxt, j)
                    if tail:
                        tail0(prev, j)
                    if ahead and j == 3:
                        input_stats(nxt2)
                    if ahead and j == 5:
                        input_rows(nxt2)
                if back:
                    normalise(b)
                if tail:
                    router(prev, xp[:], 5, E)

            def step1(b, fr, ahead, back, tail):
                nxt, nxt2, prev, prev2 = b.plus(1), b.plus(2), b.plus(-1), b.plus(-2)
                ends = tail and prev2.low >= 0
                if fr:
                    masked_queries(nxt)
                if tail:
                    residual(prev)
                    residual_stats(prev)
                    tail1a(prev)
                for j in range(NP):
                    if fr:
                        maxima(nxt, j)
                    if tail and j == 0:
                        tail1c(prev)
                    if ends and j == 1:
                        end1(prev2, 0)
                    if ahead and j == 1:
                        input_stats(nxt2)
                    if ahead and j == 2:
                        input_rows(nxt2)
                    if tail and j == 2:
                        take_product(prev, True, prev.low >= 2)
                    if ends and j == 2:
                        end1(prev2, 1)
                    if ends and j == 2:
                        end1(prev2, 2)
                if back:
                    normalise(b)
                if tail:
                    tail1b(prev)

            step = (step0, step1)[layer]
            dve.wait_ge(loaded, FIRST_LOADED)
            if layer == 0:
                dve.wait_ge(x_loaded, 16)
            input_stats(fixed(0))
            input_rows(fixed(0))
            run_dve(dve, step, link, dve_own, OWN_PER_ROUND[layer])
            if layer == 1:
                end1(fixed(NB - 1), 0)
                end1(fixed(NB - 1), 1)
                take_product(fixed(NB), False, True)
                end1(fixed(NB - 1), 2)
                take_product(fixed(NB + 1), False, True)

    end_stage(nc, sems)


def run_dve(dve, step, link, own, per):
    def peeled(t):
        step(fixed(t + 2).plus(-2), 0 <= t + 1 < NB, t + 2 < NB, 0 <= t < NB, 0 <= t - 1 < NB)

    for t in range(-1, LOOP_FROM):
        peeled(t)
    with dve.Fori(LOOP_FROM // 2, LOOP_TO // 2) as i:
        link.sem, link.base, link.n = own[1], (i - LOOP_FROM // 2) * per, 0
        for p in range(2):
            step(Batch(i, p, LOOP_FROM + p), True, True, True, True)
        assert link.n == per, link.n
    link.sem, link.base, link.n = own[2], 0, 0
    for t in range(LOOP_TO, NB + 1):
        peeled(t)


OWN_PER_ROUND = (32, 26)


def routing(nc, layer, t, env):
    NT = (NT0, NT1)[layer]
    tag = f"r{layer}_"
    BE = NB * E
    sems = []
    with ExitStack() as ctx:
        def sb(name, shape, dt=F32):
            return ctx.enter_context(nc.sbuf_tensor(tag + name, shape, dt))

        def sem(name):
            return stage_semaphore(nc, sems, tag + name)

        before = sb("before", [LQ, LQ])
        ones = sb("ones", [LQ, 128])
        onesr = sb("onesr", [128, NB])
        pref = sb("pref", [128, E])
        starts = sb("starts", [128, NTMAX])
        tile_no = sb("tile_no", [128, NTMAX])
        top = sb("top", [LQ, NB])
        w = sb("w", [LQ, NB, E])
        pr = sb("pr", [LQ, NB, E])
        M = [sb(f"M{k}", [LQ, NB, E]) for k in range(2)]
        MM = sb("MM", [LQ, NB, E])
        pos = sb("pos", [LQ, NB, E])
        tot = sb("tot", [128, NB, E])
        upto = sb("upto", [128, NB, E])
        cmp_ = sb("cmp", [128, E, NTMAX])
        cmp2 = sb("cmp2", [128, NTMAX, E])
        ntile = sb("ntile", [128, E])
        tend = sb("tend", [128, E])
        tbase = sb("tbase", [128, E])
        fl = sb("fl", [128, NTMAX])
        val = [sb(f"val{k}", [LQ, NB]) for k in range(2)]
        den = sb("den", [LQ, NB])
        tile_i = sb("tile_i", [LQ, NB], I32)
        row_i = sb("row_i", [LQ, NB], I32)
        row_no = sb("row_no", [LQ, 128])
        seq_no = sb("seq_no", [LQ, NB])
        tok_no = sb("tok_no", [LQ, 1])
        in_row = [sb(f"in_row{k}", [LQ, NB, 128], BF16) for k in range(layer + 1)]
        in_tile = [sb(f"in_tile{k}", [LQ, NB, 3, NT], BF16) for k in range(layer + 1)]
        tok_f = sb("tok_f", [128, NT])
        seq_f = sb("seq_f", [128, NT])
        second = sb("second_choice", [128, NT])
        spare = sb("spare", [128, 1])
        PS = ctx.enter_context(nc.psum_tensor(tag + "PS", [128, 3, 512], F32))

        loaded = sem("loaded")
        own = sem("own")
        act_ready = sem("act_ready")
        act_done = sem("act_done")
        mask_ready = sem("mask_ready")
        counted = sem("counted")
        slots_ready = sem("slots_ready")
        listed = sem("listed")
        share_ready = sem("share_ready")
        shares_stored = sem("shares_stored")
        consts = [(before, t["before"]), (pref, t["pref"]), (starts, t["starts"]), (tile_no, t["tile_no"]),
                  (row_no, t["row_no"]), (seq_no, t["seq_no"]), (tok_no, t["tok_no"]), (spare, t["spare"])]
        block = ctx.enter_context(nc.Block())
        AFF = env["aff"]

        @block.sync
        def _(sp):
            for dst, src in consts:
                sp.dma_start(dst[:], src).then_inc(loaded, 16)
            for dst, src in env["second"]:
                sp.dma_start(dst, src).then_inc(env["second_loaded"], 16)
            if layer == 1:
                sp.wait_ge(share_ready, 2)
                for k in range(2):
                    sp.dma_start(t["shares"][k * TOK:(k + 1) * TOK, :].rearrange("(q b) o -> q (b o)", q=LQ),
                                 env["share"][k][:]).then_inc(shares_stored, 16)
                sp.wait_ge(shares_stored, 32)

        @block.scalar
        def _(act):
            act.wait_ge(act_ready, 1)
            if layer == 0:
                nc.scalar.activation(env["alpha"][:], top[:], ACT.Sigmoid).then_inc(act_done, 1)
            else:
                nc.scalar.activation(pr[:], w[:], ACT.Exp).then_inc(act_done, 1)

        @block.tensor
        def _(pe):
            pe.wait_ge(mask_ready, 1)
            nc.tensor.matmul(PS[0:LQ, 0, 0:BE], before[:], MM[:].rearrange("q b e -> q (b e)"),
                             start=True, stop=True)
            nc.tensor.matmul(PS[:, 1, 0:BE], ones[:], MM[:].rearrange("q b e -> q (b e)"),
                             start=True, stop=True).then_inc(counted, 1)
            for k in range(layer + 1):
                pe.wait_ge(slots_ready, k + 1)
                for b in range(NB):
                    last = nc.tensor.matmul(PS[:, 2, 0:3 * NT], in_row[k][:, b, :],
                                            in_tile[k][:, b].rearrange("q a j -> q (a j)"),
                                            start=(k == 0 and b == 0), stop=(k == layer and b == NB - 1))
            last.then_inc(listed, 1)

        @block.vector
        def _(dve):
            V_ = nc.vector
            link = Links(dve, own)

            def over_e(x):
                return x[:].unsqueeze(2).to_broadcast([x.shape[0], x.shape[1], E])

            def over_b(x, n):
                return x[0:n, :].unsqueeze(1).to_broadcast([n, NB, E])

            def first_max(k, src):
                link(V_.tensor_reduce(top[:], src, AX_X, ALU.max))
                link(V_.tensor_tensor(w[:], src, over_e(top), ALU.is_equal))
                link(V_.tensor_tensor(w[:], w[:], over_b(pref, LQ), ALU.mult))
                link(V_.tensor_reduce(den[:], w[:], AX_X, ALU.max))
                link(V_.tensor_tensor(M[k][:], w[:], over_e(den), ALU.is_equal))

            dve.wait_ge(loaded, 16 * len(consts))
            link(V_.memset(ones[:], 1.0))
            link(V_.memset(onesr[:], 1.0))
            if layer == 0:
                first_max(0, AFF[:])
                V_.tensor_copy(top[:], top[:]).then_inc(act_ready, 1)
                V_.tensor_copy(MM[:], M[0][:]).then_inc(mask_ready, 1)
            else:
                link(V_.tensor_reduce(top[:], AFF[:], AX_X, ALU.max))
                V_.tensor_tensor(w[:], AFF[:], over_e(top), ALU.subtract).then_inc(act_ready, 1)
                dve.wait_ge(act_done, 1)
                link(V_.tensor_reduce(den[:], pr[:], AX_X, ALU.add))
                link(V_.reciprocal(den[:], den[:]))
                link(V_.tensor_tensor(pr[:], pr[:], over_e(den), ALU.mult))
                first_max(0, pr[:])
                link(V_.tensor_copy(val[0][:], top[:]))
                link(V_.scalar_tensor_tensor(pr[:], M[0][:], -2.0, pr[:], ALU.mult, ALU.add))
                first_max(1, pr[:])
                link(V_.tensor_copy(val[1][:], top[:]))
                link(V_.tensor_tensor(MM[:], M[0][:], M[1][:], ALU.add))
                V_.tensor_tensor(den[:], val[0][:], val[1][:], ALU.add).then_inc(mask_ready, 1)
                dve.wait_ge(mask_ready, 1)
                link(V_.tensor_scalar(den[:], den[:], 1e-9, None, ALU.add))
                link(V_.reciprocal(den[:], den[:]))
                for k in range(2):
                    V_.tensor_tensor(env["share"][k][:], val[k][:], den[:], ALU.mult).then_inc(share_ready, 1)
                dve.wait_ge(share_ready, 2)
            dve.wait_ge(counted, 1)
            link(V_.tensor_copy(tot[:].rearrange("p b e -> p (b e)"), PS[:, 1, 0:BE]))
            for e in range(E):
                link(V_.tensor_tensor_scan(upto[:, :, e], onesr[:], tot[:, :, e], 0.0, ALU.mult, ALU.add))
            link(V_.tensor_tensor(cmp_[:], upto[:, NB - 1, :].unsqueeze(2).to_broadcast([128, E, NTMAX]),
                                  starts[:].unsqueeze(1).to_broadcast([128, E, NTMAX]), ALU.is_gt))
            link(V_.tensor_reduce(ntile[:], cmp_[:], AX_X, ALU.add))
            link(V_.tensor_tensor_scan(tend[:], onesr[:, 0:E], ntile[:], 0.0, ALU.mult, ALU.add))
            link(V_.tensor_tensor(tbase[:], tend[:], ntile[:], ALU.subtract))
            link(V_.tensor_scalar(tbase[:], tbase[:], 128.0, None, ALU.mult))
            link(V_.tensor_tensor(cmp2[:], tile_no[:].unsqueeze(2).to_broadcast([128, NTMAX, E]),
                                  tend[:].unsqueeze(1).to_broadcast([128, NTMAX, E]), ALU.is_ge))
            link(V_.tensor_reduce(fl[:], cmp2[:], AX_X, ALU.add))
            link(V_.tensor_scalar(fl[:], fl[:], float(E - 1), None, ALU.min))
            link(V_.tensor_copy(env["tile_e"][:], fl[:]))
            link(V_.tensor_tensor(upto[:], upto[:], tot[:], ALU.subtract))
            link(V_.tensor_tensor(pos[:].rearrange("q b e -> q (b e)"), PS[0:LQ, 0, 0:BE],
                                  upto[0:LQ].rearrange("q b e -> q (b e)"), ALU.add))
            link(V_.tensor_tensor(pos[:], pos[:], over_b(tbase, LQ), ALU.add))
            for k in range(layer + 1):
                link(V_.tensor_tensor(w[:], pos[:], M[k][:], ALU.mult))
                link(V_.tensor_reduce(den[:], w[:], AX_X, ALU.add))
                link(V_.tensor_copy(env["slots"][k][:], den[:]))
                link(V_.tensor_scalar(tile_i[:], env["slots"][k][:], 7, None, ALU.logical_shift_right))
                link(V_.tensor_scalar(row_i[:], env["slots"][k][:], 127, None, ALU.bitwise_and))
                link(V_.tensor_tensor(in_row[k][:], row_no[:].unsqueeze(1).to_broadcast([LQ, NB, 128]),
                                      row_i[:].unsqueeze(2).to_broadcast([LQ, NB, 128]), ALU.is_equal))
                link(V_.tensor_tensor(in_tile[k][:, :, 2, :],
                                      tile_no[0:LQ, 0:NT].unsqueeze(1).to_broadcast([LQ, NB, NT]),
                                      tile_i[:].unsqueeze(2).to_broadcast([LQ, NB, NT]), ALU.is_equal))
                if k == 1:
                    link(V_.tensor_scalar(seq_no[:], seq_no[:], float(NB), None, ALU.add))
                V_.tensor_tensor(in_tile[k][:, :, 0, :], in_tile[k][:, :, 2, :],
                                 seq_no[:].unsqueeze(2).to_broadcast([LQ, NB, NT]), ALU.mult)
                V_.tensor_scalar(in_tile[k][:, :, 1, :], in_tile[k][:, :, 2, :], tok_no[:], None, ALU.mult
                                 ).then_inc(slots_ready, 1)
                dve.wait_ge(slots_ready, k + 1)
            dve.wait_ge(listed, 1)
            link(V_.tensor_copy(seq_f[:], PS[:, 2, 0:NT]))
            if layer == 1:
                link(V_.tensor_scalar(second[:], seq_f[:], float(NB), None, ALU.is_ge))
                link(V_.scalar_tensor_tensor(tok_f[:], PS[:, 2, NT:2 * NT], float(NB), seq_f[:], ALU.mult, ALU.add))
                link(V_.scalar_tensor_tensor(env["pairs"][:, 0:NT], second[:], float(TOK - NB), tok_f[:],
                                             ALU.mult, ALU.add))
                link(V_.scalar_tensor_tensor(seq_f[:], second[:], float(-NB), seq_f[:], ALU.mult, ALU.add))
            link(V_.tensor_copy(tok_f[:], PS[:, 2, NT:2 * NT]))
            link(V_.scalar_tensor_tensor(tok_f[:], seq_f[:], float(LQ), tok_f[:], ALU.mult, ALU.add))
            link(V_.tensor_copy(env["toks"][:, 0:NT], tok_f[:]))
            if layer == 1:
                link(V_.tensor_scalar(seq_f[:], PS[:, 2, 2 * NT:3 * NT], -1.0, 1.0, ALU.mult, ALU.add))
                link(V_.tensor_scalar(seq_f[:], seq_f[:], spare[:], None, ALU.mult))
                link(V_.tensor_tensor(env["rows_to"][:, 0:NT], seq_f[:], tok_f[:], ALU.add))
            if layer == 0:
                dve.wait_ge(act_done, 1)

    end_stage(nc, sems)


def expert_tiles(nc, layer, t, env):
    NT = (NT0, NT1)[layer]
    G = FC if layer == 0 else FC // 2
    SECOND = 16 * len(env["second"])
    tag = f"e{layer}_"
    sems = []
    with ExitStack() as ctx:
        def sb(name, shape, dt=F32):
            return ctx.enter_context(nc.sbuf_tensor(tag + name, shape, dt))

        def sem(name):
            return stage_semaphore(nc, sems, tag + name)

        w1 = env["w1"]
        ident = sb("ident", [128, 128])
        if layer == 0:
            w2 = env["second_buf"]
            lng = sb("lng", [128, E * DC])
            lnb = sb("lnb", [128, E * DC])
            b1 = sb("b1", [128, E * FC])
            b2 = sb("b2", [128, E, D])
        else:
            wo = sb("wo", [128, G, D])
            b1 = env["second_buf"]
            b2 = sb("b2", [128, D])
            sidx = [sb(f"sidx{p}", [128, 1], I32) for p in range(2)]
            ridx = sb("ridx", [128, 1], I32)
            share = [sb(f"share{p}", [128, 1]) for p in range(2)]
            ab = sb("ab", [128, F])
            sg = sb("sg", [128, GH])
        gidx = sb("gidx", [128, 1], I32)
        xs = sb("xs", [128, D])
        xT = sb("xT", [128, DC, 128])
        hs = sb("hs", [128, F if layer == 0 else GH])
        hT = sb("hT", [128, G, 128])
        y = [sb(f"y{p}", [128, D]) for p in range(2)]
        PX = ctx.enter_context(nc.psum_tensor(tag + "PX", [128, 512], F32))
        PH = ctx.enter_context(nc.psum_tensor(tag + "PH", [128, 2, 512], F32))
        PT = ctx.enter_context(nc.psum_tensor(tag + "PT", [128, 2, 4, 128], F32))
        PY = ctx.enter_context(nc.psum_tensor(tag + "PY", [128, 512], F32))

        small_loaded = sem("small_loaded")
        turns = env["pool_turns"]
        idx_ready = sem("idx_ready")
        rows_loaded = sem("rows_loaded")
        x_ps = sem("x_ps")
        xT_ready = sem("xT_ready")
        h_ps = sem("h_ps")
        h_read = sem("h_read")
        sig_in = sem("sig_in")
        sig_done = sem("sig_done")
        h_ready = sem("h_ready")
        hT_ps = sem("hT_ps")
        hT_act = sem("hT_act")
        hT_dve = sem("hT_dve")
        y_ps = sem("y_ps")
        y_ready = sem("y_ready")
        y_sum = sem("y_sum")
        sums_started = sem("sums_started")
        out_stored = sem("out_stored")
        sidx_ready = sem("sidx_ready")
        ridx_ready = sem("ridx_ready")
        share_loaded = [sem(f"share_loaded{p}") for p in range(2)]
        y_stored = [sem(f"y_stored{p}") for p in range(2)]

        small = [(ident, t["ident"])]
        if layer == 0:
            small += [(lng, t["lng"]), (lnb, t["lnb"]), (b1, t["b1"]), (b2, t["b2"].partition_broadcast(128))]
        else:
            small += [(wo, t["wo"]), (b2, t["b2"].partition_broadcast(128))]
        block = ctx.enter_context(nc.Block())

        @block.sync
        def _(sp):
            for dst, src in small:
                sp.dma_start(dst[:], src).then_inc(small_loaded, 16)

            if layer == 1:
                sp.dma_start(t["sums"][0:TOK, :].rearrange("(b q) d -> q b d", q=LQ), env["X"][:]
                             ).then_inc(sums_started, 16)
                sp.dma_start(t["sums"][TOK:TOK + 128, :], t["keep"][0:128, :]).then_inc(sums_started, 16)
                sp.wait_ge(y_stored[0], 16 * ((NT + 1) // 2))
                sp.wait_ge(y_stored[1], 16 * (NT // 2))
                for i in range(2):
                    half = slice(i * TOK // 2, (i + 1) * TOK // 2)
                    sp.dma_start(t["out_rows"][half, :], t["sums"][half, :]).then_inc(out_stored, 16)
                sp.wait_ge(out_stored, 32)
                return

            def store(j, p, r):
                sp.wait_ge(y_ready, j + 1)
                sp.dma_start(t["ys"][bass.ds(j * 128, 128), :], y[p][:]).then_inc(y_stored[p], 16)

            with sp.Fori(0, NT // 2) as i:
                for p in range(2):
                    store(i * 2 + p, p, i)
            if NT % 2:
                store(NT - 1, 0, NT // 2)
            sp.wait_ge(y_stored[0], 16 * ((NT + 1) // 2))
            sp.wait_ge(y_stored[1], 16 * (NT // 2))

        @block.gpsimd
        def _(pool):
            def gather(j, first):
                if not first:
                    pool.wait_ge(x_ps, j)
                pool.sem_inc(turns, 1)
                nc.gpsimd.tensor_copy(gidx[:], env["toks"][:, bass.ds(j, 1)]).then_inc(idx_ready, 1)
                pool.wait_ge(idx_ready, j + 1)
                pool.sem_inc(turns, 1)
                nc.gpsimd.indirect_dma_start(xs[:], None, t["keep"], bass.IndirectOffsetOnAxis(gidx[:], 0)
                                             ).then_inc(rows_loaded, 16)

            def gather_shares(j, p, low):
                if low >= 2:
                    pool.wait_ge(y_ready, j - 1)
                pool.sem_inc(turns, 1)
                nc.gpsimd.tensor_copy(sidx[p][:], env["pairs"][:, bass.ds(j, 1)]).then_inc(sidx_ready, 1)
                pool.wait_ge(sidx_ready, j + 1)
                pool.sem_inc(turns, 1)
                nc.gpsimd.indirect_dma_start(share[p][:], None, t["shares"], bass.IndirectOffsetOnAxis(sidx[p][:], 0)
                                             ).then_inc(share_loaded[p], 16)

            def add_rows(j, p, r, low):
                pool.wait_ge(y_ready, j + 1)
                if low == 0:
                    pool.wait_ge(sums_started, 32)
                else:
                    pool.wait_ge(y_stored[1 - p], r * 16 + 16 * p)
                pool.sem_inc(turns, 1)
                nc.gpsimd.tensor_copy(ridx[:], env["rows_to"][:, bass.ds(j, 1)]).then_inc(ridx_ready, 1)
                pool.wait_ge(ridx_ready, j + 1)
                pool.sem_inc(turns, 1)
                nc.gpsimd.indirect_dma_start(t["sums"], bass.IndirectOffsetOnAxis(ridx[:], 0), y[p][:], None,
                                             compute_op=ALU.add).then_inc(y_stored[p], 16)

            gather(0, True)
            if layer == 0:
                with pool.Fori(1, NT) as j:
                    gather(j, False)
            else:
                gather(1, False)
                for j in range(2, 6):
                    gather(j, False)
                    gather_shares(j - 2, j % 2, j - 2)
                    if j >= 4:
                        add_rows(j - 4, j % 2, 0, j - 4)
                with pool.Fori(3, NT // 2) as i:
                    for p in range(2):
                        gather(i * 2 + p, False)
                        gather_shares(i * 2 + (p - 2), p, 2)
                        add_rows(i * 2 + (p - 4), p, i - 2, 1)
                for j in range(NT // 2 * 2, NT + 2):
                    if j < NT:
                        gather(j, False)
                    gather_shares(j - 2, j % 2, 2)
                    add_rows(j - 4, j % 2, j // 2 - 2, 1)
                for j in range(NT - 2, NT):
                    add_rows(j, j % 2, j // 2, 1)

        def expert_of(engine, j):
            return engine.value_load(env["tile_e"][0:1, bass.ds(j, 1)], min_val=0, max_val=E - 1)

        @block.tensor
        def _(pe):
            def rows(j, first):
                pe.wait_ge(rows_loaded, j * 16 + 16)
                if not first:
                    pe.wait_ge(xT_ready, j)
                for c in range(DC):
                    last = nc.tensor.transpose(PX[:, c * 128:(c + 1) * 128], xs[:, c * 128:(c + 1) * 128], ident[:])
                last.then_inc(x_ps, 1)

            def up(j, first):
                e = expert_of(pe, j)
                pe.wait_ge(xT_ready, j + 1)
                if not first:
                    pe.wait_ge(h_ready if layer == 0 else h_read, j)
                for h in range(2):
                    for c in range(DC):
                        rhs = w1[:, bass.ds(e, 1), c, h * 512:(h + 1) * 512].rearrange("p o f -> p (o f)")
                        last = nc.tensor.matmul(PH[:, h, :], xT[:, c, :], rhs, start=(c == 0), stop=(c == DC - 1))
                last.then_inc(h_ps, 1)

            def turn(j, first):
                pe.wait_ge(h_ready, j + 1)
                if not first:
                    pe.wait_ge(hT_act, j)
                    if layer == 0:
                        pe.wait_ge(hT_dve, j)
                for g in range(G):
                    last = nc.tensor.transpose(PT[:, g // 4, g % 4, :], hs[:, g * 128:(g + 1) * 128], ident[:])
                last.then_inc(hT_ps, 1)

            def down(j, first):
                if layer == 0:
                    e = expert_of(pe, j)
                pe.wait_ge(hT_act, j + 1)
                if layer == 0:
                    pe.wait_ge(hT_dve, j + 1)
                if not first:
                    pe.wait_ge(y_sum if layer else y_ready, j)
                for g in range(G):
                    rhs = wo[:, g, :] if layer else w2[:, bass.ds(e, 1), g, :].rearrange("p o f -> p (o f)")
                    last = nc.tensor.matmul(PY[:, 0:D], hT[:, g, :], rhs, start=(g == 0), stop=(g == G - 1))
                last.then_inc(y_ps, 1)

            pe.wait_ge(small_loaded, 16 * len(small))
            rows(0, True)
            up(0, True)
            rows(1, False)
            if layer == 1:
                up(1, False)
                turn(0, True)
                rows(2, False)
                with pe.Fori(2, NT - 1) as j:
                    up(j, False)
                    turn(j - 1, False)
                    rows(j + 1, False)
                    down(j - 2, False)
                up(NT - 1, False)
                turn(NT - 2, False)
                down(NT - 3, False)
                turn(NT - 1, False)
                down(NT - 2, False)
                down(NT - 1, False)
                return
            turn(0, True)
            up(1, False)
            rows(2, False)
            pe.wait_ge(env["second_loaded"], SECOND)
            down(0, True)
            with pe.Fori(1, NT - 2) as j:
                turn(j, False)
                up(j + 1, False)
                rows(j + 2, False)
                down(j, False)
            turn(NT - 2, False)
            up(NT - 1, False)
            down(NT - 2, False)
            turn(NT - 1, False)
            down(NT - 1, False)

        @block.scalar
        def _(act):
            def tile(j, first):
                if layer == 0:
                    act.wait_ge(h_ps, j + 1)
                    if not first:
                        act.wait_ge(hT_ps, j)
                    nc.scalar.activation(hs[:, 0:512], PH[:, 0, :], ACT.Copy)
                    nc.scalar.activation(hs[:, 512:F], PH[:, 1, :], ACT.Copy).then_inc(h_ready, 1)
                    e = expert_of(act, j)
                    act.wait_ge(hT_ps, j + 1)
                    if not first:
                        act.wait_ge(y_ps, j)
                    for g in range(4):
                        a = nc.scalar.activation(hT[:, g, :], PT[:, 0, g, :], ACT.Relu,
                                                 bias=b1[:, bass.ds(e * FC + g, 1)])
                    a.then_inc(hT_act, 1)
                else:
                    act.wait_ge(sig_in, j + 1)
                    nc.scalar.activation(sg[:], ab[:, GH:F], ACT.Sigmoid).then_inc(sig_done, 1)
                    act.wait_ge(hT_ps, j + 1)
                    if not first:
                        act.wait_ge(y_ps, j)
                    nc.scalar.activation(hT[:], PT[:, 0], ACT.Copy).then_inc(hT_act, 1)

            act.wait_ge(small_loaded, 16 * len(small))
            tile(0, True)
            with act.Fori(1, NT) as j:
                tile(j, False)

        @block.vector
        def _(dve):
            V_ = nc.vector

            def columns(j, first):
                if layer == 0:
                    e = expert_of(dve, j)
                dve.wait_ge(x_ps, j + 1)
                if not first:
                    dve.wait_ge(h_ps, j)
                if layer == 0:
                    for c in range(DC):
                        a = V_.tensor_scalar(xT[:, c, :], PX[:, c * 128:(c + 1) * 128],
                                             lng[:, bass.ds(e * DC + c, 1)], lnb[:, bass.ds(e * DC + c, 1)],
                                             ALU.mult, ALU.add)
                else:
                    a = V_.tensor_copy(xT[:].rearrange("p c q -> p (c q)"), PX[:, 0:D])
                a.then_inc(xT_ready, 1)

            def hidden(j, first):
                e = expert_of(dve, j)
                dve.wait_ge(hT_ps, j + 1)
                if not first:
                    dve.wait_ge(y_ps, j)
                for g in range(4, G):
                    a = V_.tensor_scalar(hT[:, g, :], PT[:, 1, g - 4, :], b1[:, bass.ds(e * FC + g, 1)], 0.0,
                                         ALU.add, ALU.max)
                a.then_inc(hT_dve, 1)

            def biased(j, first):
                e = expert_of(dve, j)
                dve.wait_ge(h_ps, j + 1)
                bias = b1[:, bass.ds(e, 1), :].rearrange("p o f -> p (o f)")
                if not first:
                    dve.wait_ge(h_ready, j)
                V_.tensor_tensor(ab[:, GH:F], PH[:, 1, :], bias[:, GH:F], ALU.add).then_inc(sig_in, 1)
                V_.tensor_tensor(ab[:, 0:GH], PH[:, 0, :], bias[:, 0:GH], ALU.add).then_inc(h_read, 1)

            def gated(j, first):
                dve.wait_ge(h_read, j + 1)
                dve.wait_ge(sig_done, j + 1)
                if not first:
                    dve.wait_ge(hT_ps, j)
                V_.tensor_tensor(hs[:], ab[:, 0:GH], sg[:], ALU.mult).then_inc(h_ready, 1)

            def finish(j, p, r, low):
                if layer == 0:
                    e = expert_of(dve, j)
                dve.wait_ge(y_ps, j + 1)
                if low >= 2:
                    dve.wait_ge(y_stored[p], r * 16)
                row = b2[:, bass.ds(e, 1), :].rearrange("p o f -> p (o f)") if layer == 0 else b2[:]
                if layer == 0:
                    V_.tensor_tensor(y[p][:], PY[:, 0:D], row, ALU.add).then_inc(y_ready, 1)
                else:
                    V_.tensor_tensor(y[p][:], PY[:, 0:D], row, ALU.add).then_inc(y_sum, 1)
                    dve.wait_ge(y_sum, j + 1)
                    dve.wait_ge(share_loaded[p], r * 16 + 16)
                    V_.tensor_scalar(y[p][:], y[p][:], share[p][:], None, ALU.mult).then_inc(y_ready, 1)

            dve.wait_ge(small_loaded, 16 * len(small))
            if layer == 1:
                dve.wait_ge(env["second_loaded"], SECOND)
            columns(0, True)
            columns(1, False)
            if layer == 0:
                hidden(0, True)
                columns(2, False)
                finish(0, 0, 0, 0)
                hidden(1, False)
                columns(3, False)
                finish(1, 1, 0, 1)
                with dve.Fori(1, (NT - 2) // 2) as i:
                    for p in range(2):
                        j = i * 2 + p
                        hidden(j, False)
                        columns(j + 2, False)
                        finish(j, p, i, 2)
                for j in range(NT - 2 - NT % 2, NT):
                    hidden(j, False)
                    if j + 2 < NT:
                        columns(j + 2, False)
                    finish(j, j % 2, j // 2, 2)
            else:
                def tile(j, first, last):
                    biased(j, first)
                    if not last:
                        columns(j + 1, False)
                    gated(j, first)

                biased(0, True)
                gated(0, True)
                tile(1, False, False)
                for j in (2, 3):
                    tile(j, False, False)
                    finish(j - 2, j % 2, 0, j - 2)
                with dve.Fori(2, (NT - 1) // 2) as i:
                    for p in range(2):
                        tile(i * 2 + p, False, False)
                        finish(i * 2 + (p - 2), p, i - 1, 2)
                for j in range((NT - 1) // 2 * 2, NT):
                    tile(j, False, j == NT - 1)
                    finish(j - 2, j % 2, j // 2 - 1, 2)
                for j in range(NT - 2, NT):
                    finish(j, j % 2, j // 2, 2)

    end_stage(nc, sems)


def program(nc, t):
    t["keep"] = nc.dram_tensor("keep_rows", (TOK, D), F32, kind="Internal").ap()
    t["shares"] = nc.dram_tensor("token_shares", (2 * TOK, 1), F32, kind="Internal").ap()
    t["sums"] = nc.dram_tensor("sums", (TOK + 128, D), F32, kind="Internal").ap()
    t["out_rows"] = t["out"].rearrange("b q d -> (b q) d")
    with ExitStack() as ctx:
        def sb(name, shape, dt=F32):
            return ctx.enter_context(nc.sbuf_tensor(name, shape, dt))

        X = sb("X", [LQ, NB, D])
        affs = sb("affs", [LQ, NB, E])
        alpha = sb("alpha", [LQ, NB])
        share = [sb(f"share{k}", [LQ, NB]) for k in range(2)]
        slots = [sb(f"slots{k}", [LQ, NB], I32) for k in range(2)]
        toks = sb("toks", [128, NTMAX], I32)
        tile_e = sb("tile_e", [128, NTMAX], I32)
        pairs = sb("pairs", [128, NTMAX], I32)
        rows_to = sb("rows_to", [128, NTMAX], I32)
        pool_turns = ctx.enter_context(nc.semaphore("pool_turns"))
        env = {"pool_turns": pool_turns, "X": X, "aff": affs, "alpha": alpha, "share": share, "slots": slots, "toks": toks, "tile_e": tile_e,
               "pairs": pairs, "rows_to": rows_to}
        env["w1"] = sb("w1", [128, E, DC, F])
        consts = {n: t[n] for n in ("ident", "before", "pref", "starts", "tile_no", "row_no", "seq_no", "tok_no", "spare")}
        for layer in range(2):
            NT = (NT0, NT1)[layer]
            ys = nc.dram_tensor(f"tile_rows{layer}", (NT * 128, D), F32, kind="Internal").ap()
            mine = {n[3:]: a for n, a in t.items() if n.startswith(f"A{layer}_")}
            io = {"x": t["x"], "ctx": t["ctx"], "keep": t["keep"], "ys": t.get("ys"), "w1": t[f"E{layer}_w1"]}
            env["slots"] = slots[0]
            attention(nc, layer, {**consts, **io, **mine}, env)
            env["slots"] = slots
            mine = {n[3:]: a for n, a in t.items() if n.startswith(f"E{layer}_")}
            with ExitStack() as inner:
                if layer == 0:
                    second = inner.enter_context(nc.sbuf_tensor("w2", [128, E, FC, D], F32))
                    env["second"] = [(second[:, e], mine["w2"][:, e]) for e in range(E)]
                else:
                    second = inner.enter_context(nc.sbuf_tensor("b1_rows", [128, E, F], F32))
                    env["second"] = [(second[:], mine["b1"].partition_broadcast(128))]
                env["second_buf"] = second
                env["second_loaded"] = inner.enter_context(nc.semaphore(f"second_loaded{layer}"))
                shared = {n: t[n] for n in ("keep", "shares", "sums", "out_rows")}
                routing(nc, layer, {**consts, **shared}, env)
                expert_tiles(nc, layer, {**consts, **shared, "ys": ys, **mine}, env)
            t["ys"] = ys


def constants():
    import numpy as np

    p = np.arange(128)
    q = np.arange(LQ)
    rows = np.ones((128, 1), np.float32)
    return {
        "ident": np.eye(128, dtype=np.float32),
        "before": (q[:, None] < q[None, :]).astype(np.float32),
        "pref": rows * (E - np.arange(E, dtype=np.float32)),
        "starts": rows * (128 * np.arange(NTMAX, dtype=np.float32)),
        "tile_no": rows * np.arange(NTMAX, dtype=np.float32),
        "spare": (TOK + p[:, None]).astype(np.float32),
        "row_no": rows[0:LQ] * np.arange(128, dtype=np.float32),
        "seq_no": rows[0:LQ] * np.arange(NB, dtype=np.float32),
        "tok_no": q[:, None].astype(np.float32),
        "A0_mask": (p[:, None] // 16 == np.arange(8)[None, :]).astype(np.float32),
        "A1_mask": (p[:, None] // 32 == np.arange(4)[None, :]).astype(np.float32),
    }


def layouts(a):
    import numpy as np

    def chunks(w):
        return w.reshape(-1, 128, w.shape[-1]).transpose(1, 0, 2)

    def columns(v):
        return v.reshape(-1, 128).T

    kv = a["L0_xattn_Wkv"]
    bkv = a["L0_xattn_bkv"]
    d = {
        "x": a["x"],
        "ctx": a["ctx_1024"].reshape(NB, LK, DC, 128).transpose(0, 3, 2, 1),
        "A0_wq": chunks(a["L0_xattn_Wq"]), "A0_wk": chunks(kv[:, :D]), "A0_wv": chunks(kv[:, D:]),
        "A0_bq": columns(a["L0_xattn_bq"]), "A0_bk": columns(bkv[:D]), "A0_bv": bkv[D:],
        "A0_rows": a["L0_ffn_centroids"],
        "E0_lng": columns(a["L0_ffn_ln_g"]), "E0_lnb": columns(a["L0_ffn_ln_b"]),
        "E0_w1": a["L0_ffn_w1"].reshape(E, F, DC, 128).transpose(3, 0, 2, 1),
        "E0_b1": columns(a["L0_ffn_b1"]),
        "E0_w2": a["L0_ffn_w2"].reshape(E, D, FC, 128).transpose(3, 0, 2, 1),
        "E0_b2": a["L0_ffn_b2"],
        "A1_wq": chunks(a["L1_xattn_Wq"].T), "A1_wk": chunks(a["L1_xattn_Wk"].T),
        "A1_wv": chunks(a["L1_xattn_Wv"].T), "A1_wo": chunks(a["L1_xattn_Wo"].T),
        "A1_bq": columns(a["L1_xattn_bq"]), "A1_bk": columns(a["L1_xattn_bk"]), "A1_bv": a["L1_xattn_bv"],
        "A1_bq_row": a["L1_xattn_bq"], "A1_bo": a["L1_xattn_bo"],
        "A1_g0": a["L1_xattn_g0"], "A1_b0": a["L1_xattn_b0"], "A1_g1": a["L1_xattn_g1"], "A1_b1": a["L1_xattn_b1"],
        "A1_rows": chunks(a["L1_ffn_Wg"].T),
        "E1_w1": a["L1_ffn_W1"].reshape(E, F, DC, 128).transpose(3, 0, 2, 1),
        "E1_b1": a["L1_ffn_b1"],
        "E1_wo": chunks(a["L1_ffn_Wo"].T), "E1_b2": a["L1_ffn_bo"],
    }
    return {n: np.ascontiguousarray(v) for n, v in {**d, **constants()}.items()}


def kernel(**inputs):
    import numpy as np
    import concourse.bacc as bacc
    from concourse.bass_utils import run_bass_kernel_spmd

    nc = bacc.Bacc("TRN2", target_bir_lowering=False, num_devices=1)
    arrays = layouts({n: np.asarray(v) for n, v in inputs.items()})
    arrays = {f"in_{n}": v for n, v in arrays.items()}
    t = {n[3:]: nc.dram_tensor(n, v.shape, mybir.dt.from_np(v.dtype), kind="ExternalInput").ap()
         for n, v in arrays.items()}
    t["out"] = nc.dram_tensor("out", (NB, LQ, D), F32, kind="ExternalOutput").ap()
    program(nc, t)
    return run_bass_kernel_spmd(nc, [arrays], core_ids=[0]).results[0]["out"]
```
